# Optimizing a Trainium2 kernel written in Bass

```python
import numpy as np
import jax
import jax.numpy as jnp

def _softmax(x, axis=-1):
    return jax.nn.softmax(x, axis=axis)

def _gelu(x):
    return jax.nn.gelu(x, approximate=True)

def _silu(x):
    return jax.nn.silu(x)

def _sigmoid(x):
    return jax.nn.sigmoid(x)

def _layernorm(x, axis=-1, eps=1e-05):
    m = jnp.mean(x, axis=axis, keepdims=True)
    v = jnp.var(x, axis=axis, keepdims=True)
    return (x - m) / jnp.sqrt(v + eps)

def _scatter_add(tgt, idx, src, axis=0):
    return tgt.at[idx].add(src)

def _segment_sum(src, seg, n):
    return jax.ops.segment_sum(src, seg, n)
kernel_name = 'mk_adj_ffn_d1_adj_r2_242290'

def setup_inputs(seed: int=0):
    np.random.seed(seed)
    _w = jnp.asarray

    def _rec_inputs():
        import jax
        import jax.numpy as jnp
        _gk = jax.random.key(seed)
        x = 7.22e-05 + 1 * jax.random.normal(jax.random.fold_in(_gk, 1), (128, 128, 128), jnp.float32)
        _a = jax.random.bernoulli(jax.random.fold_in(_gk, 2), 0.03125, (128, 128, 128))
        _a = jnp.logical_or(_a, jnp.swapaxes(_a, -1, -2))
        _a = jnp.logical_or(_a, jnp.eye(128, dtype=bool))
        _af = _a.astype(jnp.float32)
        _af = _af * jax.random.uniform(jax.random.fold_in(_gk, 3), (128, 128, 128), jnp.float32, 0.05, 1)
        adj = _af
        return (x, adj)
    x, adj = _rec_inputs()

    def _L0_gnn_setup():
        import jax, jax.numpy as jnp
        import numpy as np
        B, K, H = (32, 512, 128)
        LN_EPS = 1e-05

        def layer_norm(x, gamma, beta):
            mu = jnp.mean(x, axis=-1, keepdims=True)
            var = jnp.mean(jnp.square(x - mu), axis=-1, keepdims=True)
            return (x - mu) * jax.lax.rsqrt(var + LN_EPS) * gamma + beta
        key = jax.random.key(seed)
        k1, k2, k3, k4 = jax.random.split(key, 4)
        x = jax.random.normal(k1, (B, K, H), dtype=jnp.float32)
        adj = jax.random.uniform(k2, (B, K, K), dtype=jnp.float32)
        s = 1.0 / np.sqrt(H)
        W_rel = jax.random.normal(k3, (H, H), dtype=jnp.float32) * s
        b_rel = jnp.zeros((H,), dtype=jnp.float32)
        W_root = jax.random.normal(k4, (H, H), dtype=jnp.float32) * s
        ln_gamma = jnp.ones((H,), dtype=jnp.float32)
        ln_beta = jnp.zeros((H,), dtype=jnp.float32)
        return {'x': x, 'adj': adj, 'W_rel': W_rel, 'b_rel': b_rel, 'W_root': W_root, 'ln_gamma': ln_gamma, 'ln_beta': ln_beta}
    _L0_gnn_all = _L0_gnn_setup()
    _L0_gnn_in = {k: v for k, v in _L0_gnn_all.items() if k in ('W_rel', 'b_rel', 'W_root', 'ln_gamma', 'ln_beta')}
    del _L0_gnn_all

    def _L0_ffn_setup():
        import jax, jax.numpy as jnp
        import numpy as np
        B, S, D, H, E, K = (8, 4096, 128, 512, 8, 2)
        key = jax.random.key(seed)
        ks = jax.random.split(key, 7)
        s_in = 1.0 / np.sqrt(D)
        s_hid = 1.0 / np.sqrt(H)
        return {'x': jax.random.normal(ks[0], (B, S, D), dtype=jnp.float32), 'Wg': jax.random.uniform(ks[1], (E, D), jnp.float32, -s_in, s_in), 'bg': jax.random.uniform(ks[2], (E,), jnp.float32, -s_in, s_in), 'W1': jax.random.uniform(ks[3], (E, H, D), jnp.float32, -s_in, s_in), 'b1': jax.random.uniform(ks[4], (E, H), jnp.float32, -s_in, s_in), 'W2': jax.random.uniform(ks[5], (E, D, H), jnp.float32, -s_hid, s_hid), 'b2': jax.random.uniform(ks[6], (E, D), jnp.float32, -s_hid, s_hid)}
    _L0_ffn_all = _L0_ffn_setup()
    _L0_ffn_in = {k: v for k, v in _L0_ffn_all.items() if k in ('Wg', 'bg', 'W1', 'b1', 'W2', 'b2')}
    del _L0_ffn_all
    return {'x': x, 'adj': adj, 'L0_gnn_W_rel': _L0_gnn_in['W_rel'], 'L0_gnn_b_rel': _L0_gnn_in['b_rel'], 'L0_gnn_W_root': _L0_gnn_in['W_root'], 'L0_gnn_ln_gamma': _L0_gnn_in['ln_gamma'], 'L0_gnn_ln_beta': _L0_gnn_in['ln_beta'], 'L0_ffn_Wg': _L0_ffn_in['Wg'], 'L0_ffn_bg': _L0_ffn_in['bg'], 'L0_ffn_W1': _L0_ffn_in['W1'], 'L0_ffn_b1': _L0_ffn_in['b1'], 'L0_ffn_W2': _L0_ffn_in['W2'], 'L0_ffn_b2': _L0_ffn_in['b2']}

def reference(x, adj, L0_gnn_W_rel, L0_gnn_b_rel, L0_gnn_W_root, L0_gnn_ln_gamma, L0_gnn_ln_beta, L0_ffn_Wg, L0_ffn_bg, L0_ffn_W1, L0_ffn_b1, L0_ffn_W2, L0_ffn_b2):
    import jax
    import jax.numpy as jnp

    def _L0_gnn_ref(x, adj, W_rel, b_rel, W_root, ln_gamma, ln_beta):
        import jax, jax.numpy as jnp
        import numpy as np
        B, K, H = (32, 512, 128)
        LN_EPS = 1e-05

        def layer_norm(x, gamma, beta):
            mu = jnp.mean(x, axis=-1, keepdims=True)
            var = jnp.mean(jnp.square(x - mu), axis=-1, keepdims=True)
            return (x - mu) * jax.lax.rsqrt(var + LN_EPS) * gamma + beta
        h = layer_norm(x, ln_gamma, ln_beta)
        agg = jnp.einsum('bij,bjh->bih', adj, h)
        conv = jnp.einsum('bkh,ho->bko', agg, W_rel) + b_rel + jnp.einsum('bkh,ho->bko', h, W_root)
        return x + jax.nn.relu(conv)

    def _L0_ffn_ref(x, Wg, bg, W1, b1, W2, b2):
        import jax, jax.numpy as jnp
        import numpy as np
        B, S, D, H, E, K = (8, 4096, 128, 512, 8, 2)
        gate_scores = jnp.einsum('bsd,ed->bse', x, Wg) + bg
        topk_scores, topk_idx = jax.lax.top_k(gate_scores, K)
        topk_probs = jax.nn.softmax(topk_scores, axis=-1)
        combine = jnp.sum(topk_probs[..., None] * jax.nn.one_hot(topk_idx, E, dtype=x.dtype), axis=-2)
        out = jnp.zeros_like(x)
        for e in range(E):
            h = jax.nn.relu(jnp.einsum('bsd,hd->bsh', x, W1[e]) + b1[e])
            y = jnp.einsum('bsh,dh->bsd', h, W2[e]) + b2[e]
            out = out + combine[..., e:e + 1] * y
        return out
    x = x + _L0_gnn_ref(_layernorm(x, axis=-1), adj, L0_gnn_W_rel, L0_gnn_b_rel, L0_gnn_W_root, L0_gnn_ln_gamma, L0_gnn_ln_beta)
    x = x + _L0_ffn_ref(_layernorm(x, axis=-1), L0_ffn_Wg, L0_ffn_bg, L0_ffn_W1, L0_ffn_b1, L0_ffn_W2, L0_ffn_b2)
    return x

_drawn_inputs = setup_inputs


def setup_inputs(seed=0):
    import zlib

    import numpy as np

    out = dict(_drawn_inputs(seed))
    spreads = {'L0_gnn_b_rel': (0.0, 0.268), 'L0_gnn_ln_gamma': (1.0, 0.2), 'L0_gnn_ln_beta': (0.0, 0.1)}
    factors = {'L0_ffn_bg': 3.484, 'L0_ffn_b1': 8.0, 'L0_ffn_b2': 7.536}
    for name, (base, spread) in spreads.items():
        noise = np.random.default_rng([zlib.crc32(name.encode()), seed]).standard_normal(out[name].shape)
        drawn = base * np.exp(spread * noise) if base else spread * noise
        out[name] = jnp.asarray(drawn.astype(out[name].dtype))
    for name, factor in factors.items():
        out[name] = (out[name] * factor).astype(out[name].dtype)
    return out
```

```python
from contextlib import ExitStack

import concourse.bass as bass
from concourse import mybir

F32 = mybir.dt.float32
F32R = mybir.dt.float32r
BF16 = mybir.dt.bfloat16
I32 = mybir.dt.int32
U32 = mybir.dt.uint32
ALU = mybir.AluOpType
ACT = mybir.ActivationFunctionType
X = mybir.AxisListType.X

EPS = 1e-5
SPARE = 512


def build_gnn_moe(nc, x, adj, w_rel, b_rel, w_root, gamma, beta, w_gate, b_gate, w1, b1, w2, b2, out):
    P = 128
    GRAPHS = x.shape[0]
    T = GRAPHS * P
    GB = 4
    GROUPS = GRAPHS // GB
    E = w_gate.shape[1]
    TOP = 2
    H = w1.shape[2]
    HC = H // P
    SLOT = 512
    SB = SLOT // P
    SLOTS = TOP * T // SLOT + E - 1
    CAP = T + SLOT
    ROWS = E * CAP + SLOT
    META_ID, META_GAP, META_OWN = P, P + 1, P + 2
    ROW = P + 3
    W1C, W2C = 2 * H + HC, 2 * H + 1
    TILES = T // SLOT

    routed = nc.dram_tensor("routed_rows", [ROWS, ROW], F32).ap()
    w1_split = nc.dram_tensor("w1_split", [E, P, W1C], F32).ap()
    w2_split = nc.dram_tensor("w2_split", [E, P, W2C], F32).ap()

    x_g = x.rearrange("(g b) t d -> g t b d", b=GB)
    adj_g = adj.rearrange("(g b) i j -> g i b j", b=GB)
    out_g = out[0:T, :].rearrange("(g b t) d -> g t b d", b=GB, t=P)

    with ExitStack() as ctx:
        def sb(name, shape, dt=F32):
            return ctx.enter_context(nc.sbuf_tensor(name, shape, dt))

        def sem(name):
            return ctx.enter_context(nc.semaphore(name))

        bank = [ctx.enter_context(nc.psum_tensor(f"bank{i}", [P, 512], F32)) for i in range(8)]
        ps_nT, ps_adjT, ps_rel, ps_conv, ps_yT, ps_gate, ps_rank = (bank[i] for i in range(7))
        ps_h = bank[0:4]
        ps_xT, ps_y, ps_back = bank[4], bank[5], bank[6]

        ident = sb("ident", [P, P])
        ones_bf = sb("ones_bf", [P, P], BF16)
        before_bf = sb("before_bf", [P, P], BF16)
        w_rel_s = sb("w_rel_s", [P, P])
        w_root_s = sb("w_root_s", [P, P])
        gamma_s = sb("gamma_s", [P, 1])
        beta_s = sb("beta_s", [P, 1])
        w_gate_s = sb("w_gate_s", [P, P])
        b_gate_s = sb("b_gate_s", [P, E])
        b_rel_s = sb("b_rel_s", [P, P])
        b_part = sb("b_part", [P, 3, P], BF16)
        b_row = sb("b_row", [P, 3, P], BF16)
        b_rest = sb("b_rest", [P, 2, P])
        b_sum = sb("b_sum", [P, P], BF16)
        b_rel3 = sb("b_rel3", [P, GB, P], BF16)
        count_i = sb("count_i", [P, P], I32)
        expert_f = sb("expert_f", [P, E])
        base_f = sb("base_f", [P, E])
        tile_f = sb("tile_f", [P, TILES])
        slot_f = sb("slot_f", [P, SLOTS])
        order_f = sb("order_f", [P, E, E])
        ids = sb("ids", [P, GRAPHS], I32)
        fill = sb("fill", [P, SB, ROW])
        fill_id = sb("fill_id", [P, SB], I32)

        x_in = sb("x_in", [P, 2, GB, P])
        adj_in = sb("adj_in", [P, 2, GB, P])
        xstat = sb("xstat", [P, GB, 6])
        xmv = sb("xmv", [P, GB, 2])
        xvar = sb("xvar", [P, 2, GB])
        xroot = sb("xroot", [P, 2, GB])
        xr = sb("xr", [P, 2, GB])
        xscale = sb("xscale", [P, 2, GB])
        n_s = sb("n_s", [P, 2, GB, P])
        xl_s = sb("xl_s", [P, 2, GB, P])
        hT = sb("hT", [P, 2, GB, P])
        adjT = sb("adjT", [P, 2, GB, P])
        rel_s = sb("rel_s", [P, 2, GB, P])
        x1_s = sb("x1_s", [P, 2, GB, P])
        ystat = sb("ystat", [P, GB, 6])
        ymv = sb("ymv", [P, GB, 2])
        yvar = sb("yvar", [P, GB])
        yroot = sb("yroot", [P, GB])
        yr = sb("yr", [P, GB])
        yshift = sb("yshift", [P, GB])
        rows_s = sb("rows_s", [P, 4, TOP, GB, ROW])
        yT = sb("yT", [P, 2, GB, P])
        score = sb("score", [P, GB, E])
        top8 = sb("top8", [P, GB, 8])
        which = sb("which", [P, GB, 8], U32)
        which_f = sb("which_f", [P, GB, TOP])
        gap = sb("gap", [P, 2, GB])
        hot = sb("hot", [P, 2, GB, TOP, E])
        mask = sb("mask", [P, 2, GB, E], BF16)
        seen = sb("seen", [P, 4, E], BF16)
        seen_add = sb("seen_add", [P, E])
        place = sb("place", [P, GB, E])
        placed = sb("placed", [P, GB, TOP, E])
        place_f = sb("place_f", [P, GB, TOP])
        place_i = sb("place_i", [P, 4, GB, TOP], I32)

        w_raw = sb("w_raw", [P, 2, 2 * H])
        w1_sp = sb("w1_sp", [P, 2, W1C])
        w2_sp = sb("w2_sp", [P, 2, W2C])

        length = sb("length", [P, E])
        over = sb("over", [P, E, TILES])
        tiles = sb("tiles", [P, E])
        upto = sb("upto", [P, E])
        tri_t = sb("tri_t", [P, E, E])
        past = sb("past", [P, SLOTS, E])
        pasted = sb("pasted", [P, SLOTS, E])
        s_exp = sb("s_exp", [P, SLOTS])
        s_start = sb("s_start", [P, SLOTS])
        s_row = sb("s_row", [P, SLOTS])
        s_live = sb("s_live", [P, SLOTS])
        s_new = sb("s_new", [P, SLOTS])
        ends_f = sb("ends_f", [P, E])
        ends = sb("ends", [P, E], I32)
        table = sb("table", [P, SLOTS + 2, 8], I32)

        xin = sb("xin", [P, 4, SB, ROW])
        w1_s = [sb(f"w1_s{i}", [P, W1C], F32R) for i in range(2)]
        w2_s = [sb(f"w2_s{i}", [P, W2C], F32R) for i in range(2)]
        x_hi = [sb(f"x_hi{i}", [P, SLOT], F32R) for i in range(2)]
        x_lo = [sb(f"x_lo{i}", [P, SLOT], F32R) for i in range(2)]
        h_s = sb("h_s", [P, HC, SLOT])
        h_hi = [[sb(f"h_hi{i}{c}", [P, SLOT], F32R) for c in range(HC)] for i in range(2)]
        h_lo = [[sb(f"h_lo{i}{c}", [P, SLOT], F32R) for c in range(HC)] for i in range(2)]
        yT_s = sb("yT_s", [P, 2, SLOT])
        y_s = sb("y_s", [P, 2, SB, P])
        row_id = sb("row_id", [P, 4, SB], I32)
        powers = sb("powers", [P, 4, SB, 2])
        denom = sb("denom", [P, SB])
        inverse = sb("inverse", [P, SB])
        weight = sb("weight", [P, 4, SB])

        params_loaded = sem("params_loaded")
        waits_passed = sem("waits_passed")
        pool_step = sem("pool_step")
        consts_ready = sem("consts_ready")
        split_ready = sem("split_ready")
        bias_ready = sem("bias_ready")
        rows_picked = sem("rows_picked")
        dve_step = sem("dve_step")
        raw_loaded = [sem(f"raw_loaded{i}") for i in range(2)]
        w_high = sem("w_high")
        w_split = sem("w_split")
        w_stored = [sem(f"w_stored{i}") for i in range(2)]
        x_loaded = [sem(f"x_loaded{i}") for i in range(2)]
        adj_loaded = [sem(f"adj_loaded{i}") for i in range(2)]
        xstat_done = sem("xstat_done")
        xmv_done = sem("xmv_done")
        xvar_done = sem("xvar_done")
        xroot_done = sem("xroot_done")
        xinv_done = sem("xinv_done")
        xscale_done = sem("xscale_done")
        n_ready = sem("n_ready")
        xl_ready = sem("xl_ready")
        nT_done = sem("nT_done")
        adjT_done = sem("adjT_done")
        hT_ready = sem("hT_ready")
        adjT_ready = sem("adjT_ready")
        rel_done = sem("rel_done")
        rel_ready = sem("rel_ready")
        conv_done = sem("conv_done")
        x1_ready = sem("x1_ready")
        x1_stored = [sem(f"x1_stored{i}") for i in range(2)]
        ystat_done = sem("ystat_done")
        ymv_done = sem("ymv_done")
        yvar_done = sem("yvar_done")
        yroot_done = sem("yroot_done")
        yinv_done = sem("yinv_done")
        yscale_done = sem("yscale_done")
        y_ready = sem("y_ready")
        yT_done = sem("yT_done")
        yT_ready = sem("yT_ready")
        row2_ready = sem("row2_ready")
        gate_done = sem("gate_done")
        score_ready = sem("score_ready")
        top_ready = sem("top_ready")
        gap_ready = sem("gap_ready")
        which_ready = sem("which_ready")
        hot_ready = sem("hot_ready")
        mask_ready = sem("mask_ready")
        added_ready = sem("added_ready")
        seen_ready = sem("seen_ready")
        rank_done = sem("rank_done")
        place_ready = sem("place_ready")
        placed_ready = sem("placed_ready")
        placef_ready = sem("placef_ready")
        meta_ready = sem("meta_ready")
        scattered = [sem(f"scattered{i}") for i in range(4)]
        lengths_done = sem("lengths_done")
        table_ready = sem("table_ready")
        fill_stored = sem("fill_stored")

        xin_loaded = [sem(f"xin_loaded{i}") for i in range(4)]
        w1_loaded = [sem(f"w1_loaded{i}") for i in range(2)]
        w2_loaded = [sem(f"w2_loaded{i}") for i in range(2)]
        xT_done = sem("xT_done")
        xhi_ready = sem("xhi_ready")
        xlo_ready = sem("xlo_ready")
        id_ready = sem("id_ready")
        powers_ready = sem("powers_ready")
        denom_ready = sem("denom_ready")
        inverse_ready = sem("inverse_ready")
        weight_ready = sem("weight_ready")
        h_done = sem("h_done")
        h_ready = sem("h_ready")
        hhi_ready = sem("hhi_ready")
        hlo_ready = sem("hlo_ready")
        yslot_done = sem("yslot_done")
        yslotT_ready = sem("yslotT_ready")
        back_done = sem("back_done")
        y_weighted = sem("y_weighted")
        added = [sem(f"added{i}") for i in range(2)]

        N_PARAMS = 7

        def at_least(eng, s, value):
            if isinstance(value, int) and value <= 0:
                return
            eng.wait_ge(s, value)

        def apart(eng):
            eng.sem_inc(waits_passed, 1)

        def num(t, c):
            return 4 * t + c

        def uses(t, c, ring):
            return t * (4 // ring) + c // ring + 1

        def pipeline(eng, step, first_full, n, lag_end):
            rounds = (n - first_full) // 4
            for i in range(first_full):
                step(0, i)
            with eng.Fori(0, rounds) as t:
                for c in range(4):
                    step(t, first_full + c)
            for i in range(first_full + 4 * rounds, n + lag_end):
                step(0, i)

        def runs(t, c, lag, n):
            i = 4 * t + c if isinstance(t, int) else None
            return i is None or 0 <= i - lag < n

        A_FULL, A_LAG = 5, 3
        B_FULL, B_LAG = 4, 2
        B_LAST = SLOTS - 1

        def run_a(eng, step):
            pipeline(eng, step, A_FULL, GROUPS - 1, 1 + A_LAG)

        def run_b(eng, step):
            pipeline(eng, step, B_FULL, B_LAST, 1 + B_LAG)

        block = ctx.enter_context(nc.Block())

        @block.sync
        def _(sp):
            for dst, src in ((w_rel_s[:, :], w_rel), (w_root_s[:, :], w_root), (gamma_s[:, :], gamma),
                             (beta_s[:, :], beta), (b_gate_s[:, :], b_gate.partition_broadcast(P)),
                             (b_rel_s[:, :], b_rel.partition_broadcast(P))):
                sp.dma_start(dst, src).then_inc(params_loaded, 16)

            def load(t, c):
                g, p = num(t, c), c % 2
                at_least(sp, xl_ready, g - 1)
                at_least(sp, n_ready, g - 1)
                sp.dma_start(x_in[:, p, :, :], x_g[g]).then_inc(x_loaded[p], 16)
                at_least(sp, adjT_done, g - 1)
                sp.dma_start(adj_in[:, p, :, :], adj_g[g]).then_inc(adj_loaded[p], 16)

            def store(t, c):
                g, p = num(t, c), c % 2
                sp.wait_ge(x1_ready, g + 1)
                sp.dma_start(out_g[g], x1_s[:, p, :, :]).then_inc(x1_stored[p], 16)

            load(0, 0)
            sp.wait_ge(consts_ready, 1)
            sp.dma_start(w_gate_s[:, 0:E], w_gate).then_inc(params_loaded, 16)

            def step(t, c):
                if runs(t, c, -1, GROUPS):
                    load(t, c + 1)
                if runs(t, c, 1, GROUPS):
                    store(t, c - 1)

            pipeline(sp, step, 3, GROUPS - 1, 2)

            sp.wait_ge(table_ready, 1)
            for e in range(E):
                end = sp.value_load(ends[0:1, e:e + 1], min_val=0, max_val=ROWS - SLOT)
                dst = routed[bass.ds(end, SLOT), :].rearrange("(j p) d -> p j d", p=P)
                sp.dma_start(dst, fill[:, :, :]).then_inc(fill_stored, 16)
            sp.dma_start(routed[E * CAP:ROWS, :].rearrange("(j p) d -> p j d", p=P),
                         fill[:, :, :]).then_inc(fill_stored, 16)
            sp.dma_start(out[T:T + SPARE, :].rearrange("(j p) d -> p j d", p=P),
                         fill[:, :, 0:P]).then_inc(fill_stored, 16)
            sp.wait_ge(fill_stored, 16 * (E + 2))
            for r in range(4):
                sp.wait_ge(scattered[r], 128 * (GROUPS // 4))
            for p in range(2):
                sp.wait_ge(w_stored[p], 32 * (E // 2))
                sp.wait_ge(x1_stored[p], 16 * (GROUPS // 2))

            BOUNDED = "part P's arithmetic keeps each value in the bounds that the shapes give"

            def step_b(t, c):
                s = num(t, c)
                at = slice(s + 2, s + 3) if isinstance(s, int) else bass.ds(s + 2, 1)
                _, (row, e1, new1, e2, new2) = nc.values_load_multi_w_load_instructions(
                    table[0:1, at, 0:5].rearrange("p a c -> p (a c)"), engines=[mybir.EngineType.SP], min_val=0, max_val=ROWS - SLOT,
                    skip_runtime_bounds_check_because=BOUNDED)
                e1, e2 = (nc.s_assert_within(e, 0, E - 1, skip_runtime_bounds_check_because=BOUNDED) for e in (e1, e2))
                new1, new2 = (nc.s_assert_within(n, 0, 1, skip_runtime_bounds_check_because=BOUNDED) for n in (new1, new2))
                if runs(t, c, -2, SLOTS):
                    r = (c + 2) % 4
                    at_least(sp, xT_done, s - 1)
                    at_least(sp, powers_ready, s - 1)
                    at_least(sp, id_ready, s - 1)
                    src = routed[bass.ds(row, SLOT), :].rearrange("(j p) d -> p j d", p=P)
                    sp.dma_start(xin[:, r, :, :], src).then_inc(xin_loaded[r], 16)
                if runs(t, c, -1, SLOTS):
                    p = (c + 1) % 2
                    at_least(sp, h_ready, HC * s)
                    sp.dma_start(w1_s[p][:, :].bitcast(F32), w1_split[bass.ds(e1, 1), :, :].rearrange("a p c -> p (a c)"),
                                 cond=new1).then_inc(w1_loaded[p], 16)
                if runs(t, c, 0, SLOTS):
                    p = c % 2
                    at_least(sp, yslotT_ready, s - 1)
                    sp.dma_start(w2_s[p][:, :].bitcast(F32), w2_split[bass.ds(e2, 1), :, :].rearrange("a p c -> p (a c)"),
                                 cond=new2).then_inc(w2_loaded[p], 16)

            step_b(0, -2)
            step_b(0, -1)
            pipeline(sp, step_b, 3, SLOTS - 2, 2)
            sp.wait_ge(added[0], 64 * ((SLOTS + 1) // 2))
            sp.wait_ge(added[1], 64 * (SLOTS // 2))

        @block.gpsimd
        def _(pool):
            nc.gpsimd.memset(w_gate_s[:, :], 0.0).then_inc(consts_ready, 1)
            nc.gpsimd.memset(ident[:, :], 0.0).then_inc(pool_step, 1)
            nc.gpsimd.memset(ones_bf[:, :], 1.0).then_inc(pool_step, 1)
            nc.gpsimd.memset(fill[:, :, :], 0.0).then_inc(pool_step, 1)
            pool.wait_ge(pool_step, 3)
            nc.gpsimd.affine_select(out=ident[:, :], in_=ident[:, :], compare_op=ALU.not_equal, fill=1.0,
                                    base=0, pattern=[[-1, P]], channel_multiplier=1).then_inc(pool_step, 1)
            nc.gpsimd.affine_select(out=before_bf[:, :], in_=ones_bf[:, :], compare_op=ALU.is_gt, fill=0.0,
                                    base=0, pattern=[[1, P]], channel_multiplier=-1).then_inc(pool_step, 1)
            nc.gpsimd.iota(ids[:, :], pattern=[[P, GRAPHS]], base=0, channel_multiplier=1).then_inc(pool_step, 1)
            nc.gpsimd.iota(fill_id[:, :], pattern=[[P, SB]], base=T, channel_multiplier=1).then_inc(pool_step, 1)
            pool.wait_ge(pool_step, 7)
            nc.gpsimd.tensor_copy(fill[:, :, META_ID:META_ID + 1].bitcast(I32),
                                  fill_id[:, :].unsqueeze(2)).then_inc(pool_step, 1)
            made = 8
            for dst, n, pattern in ((expert_f[:, :], E, [[1, E]]), (base_f[:, :], E, [[CAP, E]]),
                                    (tile_f[:, :], TILES, [[SLOT, TILES]]), (slot_f[:, :], SLOTS, [[1, SLOTS]]),
                                    (order_f[:, :, :].rearrange("p e f -> p (e f)"), E * E, [[1, E], [-1, E]])):
                nc.gpsimd.iota(count_i[:, 0:n], pattern=pattern, base=0, channel_multiplier=0).then_inc(pool_step, 1)
                made += 1
                pool.wait_ge(pool_step, made)
                nc.gpsimd.tensor_copy(dst, count_i[:, 0:n]).then_inc(pool_step, 1)
                made += 1
                pool.wait_ge(pool_step, made)
            pool.wait_ge(split_ready, 1)
            for k in range(3):
                nc.gpsimd.affine_select(out=b_row[:, k, :], in_=b_part[:, k, :], compare_op=ALU.is_equal, fill=0.0,
                                        base=-k, pattern=[[0, P]], channel_multiplier=1).then_inc(rows_picked, 1)

            def pass_weights(pair):
                for p in range(2):
                    at_least(pool, w_stored[p], 32 * pair)
                    apart(pool)
                    one = bass.ds(2 * pair + p, 1)
                    for dst, src in ((w_raw[:, p, 0:H], w1[one]), (w_raw[:, p, H:2 * H], w2[one]),
                                     (w1_sp[:, p, 2 * H:W1C], b1[one]), (w2_sp[:, p, 2 * H:W2C], b2[one])):
                        pool.dma_start(dst, src.rearrange("a p c -> p (a c)")).then_inc(raw_loaded[p], 16)
                for p in range(2):
                    e = 2 * pair + p
                    one = bass.ds(e, 1)
                    pool.wait_ge(w_split, e + 1)
                    apart(pool)
                    pool.dma_start(w1_split[one].rearrange("a p c -> p (a c)"), w1_sp[:, p, :]).then_inc(w_stored[p], 16)
                    pool.dma_start(w2_split[one].rearrange("a p c -> p (a c)"), w2_sp[:, p, :]).then_inc(w_stored[p], 16)

            pass_weights(0)
            with pool.Fori(1, E // 2) as pair:
                pass_weights(pair)

            def step(t, c):
                if runs(t, c, 3, GROUPS):
                    g, r = num(t, c - 3), (c - 3) % 4
                    pool.wait_ge(meta_ready, g + 1)
                    pool.wait_ge(row2_ready, g + 1)
                    apart(pool)
                    for b in range(GB):
                        for k in range(TOP):
                            pool.indirect_dma_start(
                                out=routed, out_offset=bass.IndirectOffsetOnAxis(ap=place_i[:, r, b, k:k + 1], axis=0),
                                in_=rows_s[:, r, k, b, :], in_offset=None).then_inc(scattered[r], 16)

            run_a(pool, step)

            def step_b(t, c):
                if runs(t, c, 2, SLOTS):
                    s, p, r = num(t, c - 2), (c - 2) % 2, (c - 2) % 4
                    pool.wait_ge(y_weighted, s + 1)
                    pool.wait_ge(id_ready, s + 1)
                    at_least(pool, added[1 - p], 64 * uses(t, c - 3, 2) if c >= 3 or not isinstance(t, int) else 0)
                    apart(pool)
                    for j in range(SB):
                        pool.indirect_dma_start(
                            out=out, out_offset=bass.IndirectOffsetOnAxis(
                                ap=row_id[:, r, j:j + 1], axis=0),
                            in_=y_s[:, p, j, :], in_offset=None, compute_op=ALU.add,
                            bounds_check=T + SPARE - 1).then_inc(added[p], 16)

            run_b(pool, step_b)

        @block.scalar
        def _(act):
            act.wait_ge(params_loaded, 16 * N_PARAMS)

            def x_root(t, c):
                act.wait_ge(xvar_done, num(t, c) + 1)
                nc.scalar.activation(xroot[:, :, :], xvar[:, :, :], ACT.Sqrt).then_inc(xroot_done, 1)

            def step(t, c):
                if runs(t, c, 0, GROUPS):
                    g, p = num(t, c), c % 2
                    act.wait_ge(nT_done, g + 1)
                    at_least(act, rel_done, g - 1)
                    at_least(act, conv_done, g - 1)
                    nc.scalar.activation(hT[:, p, :, :], ps_nT[:, :].rearrange("p (b t) -> p b t", b=GB),
                                         ACT.Identity, bias=beta_s[:, 0:1], scale=gamma_s[:, 0:1]).then_inc(hT_ready, 1)
                    act.wait_ge(adjT_done, g + 1)
                    nc.scalar.activation(adjT[:, p, :, :], ps_adjT[:, :].rearrange("p (b t) -> p b t", b=GB),
                                         ACT.Copy).then_inc(adjT_ready, 1)
                    act.wait_ge(rel_done, g + 1)
                    nc.scalar.activation(rel_s[:, p, :, :], ps_rel[:, :].rearrange("p (b t) -> p b t", b=GB),
                                         ACT.Copy).then_inc(rel_ready, 1)
                    act.wait_ge(xscale_done, g + 1)
                    act.wait_ge(x_loaded[p], 16 * uses(t, c, 2))
                    at_least(act, x1_ready, g - 1)
                    for b in range(GB):
                        last = nc.scalar.activation(xl_s[:, p, b, :], x_in[:, p, b, :], ACT.Identity,
                                                    bias=xscale[:, 1, b:b + 1], scale=xscale[:, 0, b:b + 1])
                    last.then_inc(xl_ready, 1)
                if runs(t, c, 1, GROUPS):
                    act.wait_ge(yvar_done, num(t, c - 1) + 1)
                    nc.scalar.activation(yroot[:, :], yvar[:, :], ACT.Sqrt).then_inc(yroot_done, 1)
                if runs(t, c, -1, GROUPS):
                    x_root(t, c + 1)
                if runs(t, c, 1, GROUPS):
                    g, p, r = num(t, c - 1), (c - 1) % 2, (c - 1) % 4
                    act.wait_ge(yscale_done, g + 1)
                    if not isinstance(g, int) or g >= 4:
                        at_least(act, scattered[r], 128 * (uses(t, c - 1, 4) - 1))
                    for b in range(GB):
                        last = nc.scalar.activation(rows_s[:, r, 0, b, 0:P], x1_s[:, p, b, :], ACT.Identity,
                                                    bias=yshift[:, b:b + 1], scale=yr[:, b:b + 1])
                    last.then_inc(y_ready, 1)
                    act.wait_ge(y_ready, g + 1)
                    nc.scalar.activation(rows_s[:, r, 1, :, 0:P], rows_s[:, r, 0, :, 0:P],
                                         ACT.Copy).then_inc(row2_ready, 1)
                    act.wait_ge(yT_done, g + 1)
                    at_least(act, gate_done, g - 1)
                    nc.scalar.activation(yT[:, p, :, :], ps_yT[:, :].rearrange("p (b t) -> p b t", b=GB),
                                         ACT.Copy).then_inc(yT_ready, 1)

            x_root(0, 0)
            run_a(act, step)

            def step_b(t, c):
                s = num(t, c)
                if runs(t, c, 0, SLOTS):
                    p = c % 2
                    for hc in range(HC):
                        act.wait_ge(h_done, HC * s + hc + 1)
                        at_least(act, hlo_ready, HC * (s - 1) + hc + 1)
                        nc.scalar.activation(h_s[:, hc, :], ps_h[hc][:, :], ACT.Relu,
                                             bias=w1_s[p][:, 2 * H + hc:2 * H + hc + 1].bitcast(F32)).then_inc(h_ready, 1)
                if runs(t, c, -1, SLOTS):
                    x_high(t, c + 1)
                if runs(t, c, 2, SLOTS):
                    s2, p, r = num(t, c - 2), (c - 2) % 2, (c - 2) % 4
                    act.wait_ge(back_done, s2 + 1)
                    act.wait_ge(weight_ready, s2 + 1)
                    if not isinstance(s2, int) or s2 >= 2:
                        at_least(act, added[p], 64 * (uses(t, c - 2, 2) - 1))
                    for j in range(SB):
                        last = nc.scalar.activation(y_s[:, p, j, :], ps_back[:, j * P:(j + 1) * P], ACT.Copy,
                                                    scale=weight[:, r, j:j + 1])
                    last.then_inc(y_weighted, 1)

            def x_high(t, c):
                s, p = num(t, c), c % 2
                act.wait_ge(xT_done, s + 1)
                at_least(act, h_done, HC * (s - 1))
                nc.scalar.activation(x_hi[p][:, :], ps_xT[:, :], ACT.Copy).then_inc(xhi_ready, 1)
                r = c % 4
                act.wait_ge(xin_loaded[r], 16 * uses(t, c, 4))
                at_least(act, weight_ready, s - 3)
                nc.scalar.activation(powers[:, r, :, :], xin[:, r, :, META_GAP:META_OWN + 1], ACT.Exp).then_inc(powers_ready, 1)

            x_high(0, 0)
            run_b(act, step_b)

        @block.vector
        def _(dve):
            steps = [0]

            def link(ins):
                steps[0] += 1
                ins.then_inc(dve_step, 1)
                dve.wait_ge(dve_step, steps[0])

            dve.wait_ge(params_loaded, 16 * N_PARAMS)
            link(nc.vector.tensor_copy(b_part[:, 0, :], b_rel_s[:, :]))
            link(nc.vector.tensor_tensor(b_rest[:, 0, :], b_rel_s[:, :], b_part[:, 0, :], ALU.subtract))
            link(nc.vector.tensor_copy(b_part[:, 1, :], b_rest[:, 0, :]))
            link(nc.vector.tensor_tensor(b_rest[:, 1, :], b_rest[:, 0, :], b_part[:, 1, :], ALU.subtract))
            nc.vector.tensor_copy(b_part[:, 2, :], b_rest[:, 1, :]).then_inc(split_ready, 1)
            nc.vector.memset(seen[:, 0, :], 0.0).then_inc(seen_ready, 1)
            dve.wait_ge(rows_picked, 3)
            link(nc.vector.tensor_tensor(b_sum[:, :], b_row[:, 0, :], b_row[:, 1, :], ALU.add))
            link(nc.vector.tensor_tensor(b_sum[:, :], b_sum[:, :], b_row[:, 2, :], ALU.add))
            nc.vector.tensor_copy(b_rel3[:, :, :], b_sum[:, :].unsqueeze(1).to_broadcast([P, GB, P])).then_inc(bias_ready, 1)

            def stage1_stats(t, c):
                g, p = num(t, c), c % 2
                dve.wait_ge(x_loaded[p], 16 * uses(t, c, 2))
                for b in range(GB):
                    last = nc.vector.bn_stats(xstat[:, b, :], x_in[:, p, b, :])
                last.then_inc(xstat_done, 1)
                dve.wait_ge(xstat_done, g + 1)
                apart(dve)
                for b in range(GB):
                    last = nc.vector.bn_aggr(xmv[:, b, :], xstat[:, b, :])
                last.then_inc(xmv_done, 1)
                dve.wait_ge(xmv_done, g + 1)
                at_least(dve, xroot_done, g)
                nc.vector.tensor_scalar(xvar[:, 0, :], xmv[:, :, 1], EPS, None, ALU.add)
                nc.vector.tensor_scalar(xvar[:, 1, :], xmv[:, :, 1], 1.0 + EPS, EPS * EPS, ALU.mult, ALU.add).then_inc(xvar_done, 1)

            def stage1(t, c):
                g, p = num(t, c), c % 2
                dve.wait_ge(xroot_done, g + 1)
                nc.vector.reciprocal(xr[:, :, :], xroot[:, :, :]).then_inc(xinv_done, 1)
                dve.wait_ge(xinv_done, g + 1)
                at_least(dve, xl_ready, g)
                nc.vector.tensor_scalar(xscale[:, 0, :], xr[:, 0, :], 1.0, None, ALU.add)
                nc.vector.scalar_tensor_tensor(out=xscale[:, 1, :], in0=xmv[:, :, 0], scalar=-1.0, in1=xr[:, 0, :],
                                               op0=ALU.mult, op1=ALU.mult).then_inc(xscale_done, 1)
                at_least(dve, nT_done, g - 1)
                for b in range(GB):
                    last = nc.vector.tensor_scalar(n_s[:, p, b, :], x_in[:, p, b, :], xmv[:, b, 0:1], xr[:, 1, b:b + 1],
                                                   ALU.subtract, ALU.mult)
                last.then_inc(n_ready, 1)

            def stage2_stats(t, c):
                g, p = num(t, c), c % 2
                dve.wait_ge(conv_done, g + 1)
                dve.wait_ge(xl_ready, g + 1)
                if not isinstance(g, int) or g >= 2:
                    at_least(dve, x1_stored[p], 16 * (uses(t, c, 2) - 1))
                at_least(dve, y_ready, g - 1)
                nc.vector.scalar_tensor_tensor(out=x1_s[:, p, :, :], in0=ps_conv[:, :].rearrange("p (b t) -> p b t", b=GB),
                                               scalar=0.0, in1=xl_s[:, p, :, :], op0=ALU.max, op1=ALU.add).then_inc(x1_ready, 1)
                dve.wait_ge(x1_ready, g + 1)
                for b in range(GB):
                    last = nc.vector.bn_stats(ystat[:, b, :], x1_s[:, p, b, :])
                last.then_inc(ystat_done, 1)
                dve.wait_ge(ystat_done, g + 1)
                apart(dve)
                for b in range(GB):
                    last = nc.vector.bn_aggr(ymv[:, b, :], ystat[:, b, :])
                last.then_inc(ymv_done, 1)
                dve.wait_ge(ymv_done, g + 1)
                nc.vector.tensor_scalar(yvar[:, :], ymv[:, :, 1], EPS, None, ALU.add).then_inc(yvar_done, 1)

            def stage2(t, c):
                g, p, r = num(t, c), c % 2, c % 4
                dve.wait_ge(yroot_done, g + 1)
                at_least(dve, y_ready, g)
                nc.vector.reciprocal(yr[:, :], yroot[:, :]).then_inc(yinv_done, 1)
                dve.wait_ge(yinv_done, g + 1)
                nc.vector.scalar_tensor_tensor(out=yshift[:, :], in0=ymv[:, :, 0], scalar=-1.0, in1=yr[:, :],
                                               op0=ALU.mult, op1=ALU.mult).then_inc(yscale_done, 1)

            def stage3(t, c):
                g, p, r = num(t, c), c % 2, c % 4
                dve.wait_ge(gate_done, g + 1)
                nc.vector.tensor_tensor(score[:, :, :], ps_gate[:, :].rearrange("p (b e) -> p b e", b=GB)[:, :, 0:E],
                                        b_gate_s[:, :].unsqueeze(1).to_broadcast([P, GB, E]), ALU.add).then_inc(score_ready, 1)
                dve.wait_ge(score_ready, g + 1)
                apart(dve)
                for b in range(GB):
                    last = nc.vector.max(top8[:, b, :], score[:, b, :])
                last.then_inc(top_ready, 1)
                dve.wait_ge(top_ready, g + 1)
                apart(dve)
                for b in range(GB):
                    last = nc.vector.max_index(which[:, b, :], top8[:, b, :], score[:, b, :])
                last.then_inc(which_ready, 1)
                nc.vector.tensor_tensor(gap[:, p, :], top8[:, :, 1], top8[:, :, 0], ALU.subtract).then_inc(gap_ready, 1)
                dve.wait_ge(which_ready, g + 1)
                nc.vector.tensor_copy(which_f[:, :, :], which[:, :, 0:TOP]).then_inc(hot_ready, 1)
                dve.wait_ge(hot_ready, 2 * g + 1)
                nc.vector.tensor_tensor(hot[:, p, :, :, :], which_f[:, :, :].unsqueeze(3).to_broadcast([P, GB, TOP, E]),
                                        expert_f[:, :].unsqueeze(1).unsqueeze(1).to_broadcast([P, GB, TOP, E]),
                                        ALU.is_equal).then_inc(hot_ready, 1)
                dve.wait_ge(hot_ready, 2 * g + 2)
                at_least(dve, rank_done, g - 1)
                nc.vector.tensor_tensor(mask[:, p, :, :], hot[:, p, :, 0, :], hot[:, p, :, 1, :], ALU.add).then_inc(mask_ready, 1)
                dve.wait_ge(mask_ready, g + 1)
                nc.vector.tensor_reduce(seen_add[:, :], mask[:, p, :, :].rearrange("p b e -> p e b"), X, ALU.add).then_inc(added_ready, 1)
                dve.wait_ge(added_ready, g + 1)
                at_least(dve, rank_done, g - 2)
                nc.vector.tensor_tensor(seen[:, (r + 1) % 4, :], seen[:, r, :], seen_add[:, :], ALU.add).then_inc(seen_ready, 1)

            def stage4(t, c):
                g, p, r = num(t, c), c % 2, c % 4
                dve.wait_ge(rank_done, g + 1)
                nc.vector.tensor_tensor(place[:, :, :], ps_rank[:, 0:GB * E].rearrange("p (b e) -> p b e", b=GB),
                                        base_f[:, :].unsqueeze(1).to_broadcast([P, GB, E]), ALU.add).then_inc(place_ready, 1)
                dve.wait_ge(place_ready, g + 1)
                nc.vector.tensor_tensor(placed[:, :, :, :], hot[:, p, :, :, :],
                                        place[:, :, :].unsqueeze(2).to_broadcast([P, GB, TOP, E]), ALU.mult).then_inc(placed_ready, 1)
                dve.wait_ge(gap_ready, g + 1)
                dve.wait_ge(y_ready, g + 1)
                nc.vector.tensor_copy(rows_s[:, r, :, :, META_GAP], gap[:, p, :].unsqueeze(1).to_broadcast([P, TOP, GB]))
                nc.vector.memset(rows_s[:, r, 0, :, META_OWN], 0.0)
                nc.vector.tensor_copy(rows_s[:, r, 1, :, META_OWN], gap[:, p, :])
                dve.wait_ge(placed_ready, g + 1)
                nc.vector.tensor_reduce(place_f[:, :, :], placed[:, :, :, :], X, ALU.add).then_inc(placef_ready, 1)
                one = ids[:, GB * g:GB * g + GB] if isinstance(g, int) else ids[:, bass.ds(GB * g, GB)]
                nc.vector.tensor_copy(rows_s[:, r, :, :, META_ID].bitcast(I32), one.unsqueeze(1).to_broadcast([P, TOP, GB]))
                dve.wait_ge(placef_ready, g + 1)
                nc.vector.tensor_copy(place_i[:, r, :, :], place_f[:, :, :]).then_inc(meta_ready, 1)

            def step(t, c):
                if runs(t, c, 0, GROUPS):
                    stage1(t, c)
                if runs(t, c, 3, GROUPS):
                    stage4(t, c - 3)
                if runs(t, c, 1, GROUPS):
                    stage2_stats(t, c - 1)
                if runs(t, c, -1, GROUPS):
                    stage1_stats(t, c + 1)
                if runs(t, c, 1, GROUPS):
                    stage2(t, c - 1)
                if runs(t, c, 2, GROUPS):
                    stage3(t, c - 2)
                if isinstance(t, int) and c == 2:
                    split_weights()

            def split_weights():
                with dve.Fori(0, E // 2) as pair:
                    for p in range(2):
                        e = 2 * pair + p
                        dve.wait_ge(raw_loaded[p], 64 * (pair + 1))
                        for n, sp_ in enumerate((w1_sp, w2_sp)):
                            nc.vector.tensor_copy(sp_[:, p, 0:H].bitcast(F32R), w_raw[:, p, n * H:(n + 1) * H]).then_inc(w_high, 1)
                        dve.wait_ge(w_high, 2 * (e + 1))
                        for n, sp_ in enumerate((w1_sp, w2_sp)):
                            last = nc.vector.tensor_tensor(sp_[:, p, H:2 * H].bitcast(F32R), w_raw[:, p, n * H:(n + 1) * H],
                                                           sp_[:, p, 0:H], ALU.subtract)
                        last.then_inc(w_split, 1)

            stage1_stats(0, 0)
            run_a(dve, step)

            dve.wait_ge(lengths_done, 1)
            link(nc.vector.tensor_copy(length[:, :], ps_rank[:, 0:E]))
            nc.vector.tensor_tensor(ends_f[:, :], length[:, :], base_f[:, :], ALU.add)
            link(nc.vector.tensor_tensor(over[:, :, :], length[:, :].unsqueeze(2).to_broadcast([P, E, TILES]),
                                         tile_f[:, :].unsqueeze(1).to_broadcast([P, E, TILES]), ALU.is_gt))
            link(nc.vector.tensor_reduce(tiles[:, :], over[:, :, :], X, ALU.add))
            link(nc.vector.tensor_scalar(tri_t[:, :, :], order_f[:, :, :], 0.0, None, ALU.is_ge))
            link(nc.vector.tensor_tensor(tri_t[:, :, :], tri_t[:, :, :], tiles[:, :].unsqueeze(1).to_broadcast([P, E, E]), ALU.mult))
            link(nc.vector.tensor_reduce(upto[:, :], tri_t[:, :, :], X, ALU.add))
            link(nc.vector.tensor_tensor(past[:, :, :], slot_f[:, :].unsqueeze(2).to_broadcast([P, SLOTS, E]),
                                         upto[:, :].unsqueeze(1).to_broadcast([P, SLOTS, E]), ALU.is_ge))
            link(nc.vector.tensor_reduce(s_exp[:, :], past[:, :, :], X, ALU.add))
            link(nc.vector.tensor_tensor(pasted[:, :, :], past[:, :, :], tiles[:, :].unsqueeze(1).to_broadcast([P, SLOTS, E]), ALU.mult))
            link(nc.vector.tensor_reduce(s_start[:, :], pasted[:, :, :], X, ALU.add))
            link(nc.vector.tensor_scalar(s_live[:, :], s_exp[:, :], float(E), float(SLOT), ALU.is_lt, ALU.mult))
            link(nc.vector.tensor_tensor(s_row[:, :], slot_f[:, :], s_start[:, :], ALU.subtract))
            link(nc.vector.tensor_tensor(s_row[:, :], s_row[:, :], s_live[:, :], ALU.mult))
            link(nc.vector.scalar_tensor_tensor(out=s_row[:, :], in0=s_exp[:, :], scalar=float(CAP), in1=s_row[:, :],
                                                op0=ALU.mult, op1=ALU.add))
            link(nc.vector.tensor_scalar(s_exp[:, :], s_exp[:, :], float(E - 1), None, ALU.min))
            nc.vector.memset(s_new[:, 0:2], 1.0)
            link(nc.vector.tensor_tensor(s_new[:, 2:SLOTS], s_exp[:, 2:SLOTS], s_exp[:, 0:SLOTS - 2], ALU.not_equal))
            link(nc.vector.memset(table[:, :, :], 0))
            nc.vector.tensor_copy(table[:, 0:SLOTS, 0], s_row[:, :])
            nc.vector.tensor_copy(table[:, 1:SLOTS + 1, 1], s_exp[:, :])
            nc.vector.tensor_copy(table[:, 1:SLOTS + 1, 2], s_new[:, :])
            nc.vector.tensor_copy(table[:, 2:SLOTS + 2, 3], s_exp[:, :])
            nc.vector.tensor_copy(table[:, 2:SLOTS + 2, 4], s_new[:, :])
            nc.vector.tensor_copy(ends[:, :], ends_f[:, :]).then_inc(table_ready, 1)

            def x_low(t, c):
                s, p = num(t, c), c % 2
                dve.wait_ge(xhi_ready, s + 1)
                at_least(dve, h_done, HC * (s - 1))
                nc.vector.tensor_tensor(x_lo[p][:, :], ps_xT[:, :], x_hi[p][:, :].bitcast(F32), ALU.subtract).then_inc(xlo_ready, 1)
                r = c % 4
                dve.wait_ge(xin_loaded[r], 16 * uses(t, c, 4))
                if not isinstance(s, int) or s >= 4:
                    at_least(dve, added[p], 64 * (uses(t, c, 2) - 2))
                nc.vector.tensor_copy(row_id[:, r, :], xin[:, r, :, META_ID].bitcast(I32)).then_inc(id_ready, 1)

            def step_b(t, c):
                if runs(t, c, 2, SLOTS):
                    s, p = num(t, c - 2), (c - 2) % 2
                    dve.wait_ge(yslot_done, s + 1)
                    at_least(dve, back_done, s - 1)
                    nc.vector.tensor_scalar(yT_s[:, p, :], ps_y[:, :], w2_s[p][:, 2 * H:2 * H + 1].bitcast(F32), None,
                                            ALU.add).then_inc(yslotT_ready, 1)
                if runs(t, c, 0, SLOTS):
                    s, p = num(t, c), c % 2
                    for hc in range(HC):
                        dve.wait_ge(h_ready, HC * s + hc + 1)
                        nc.vector.tensor_copy(h_hi[p][hc][:, :], h_s[:, hc, :]).then_inc(hhi_ready, 1)
                        dve.wait_ge(hhi_ready, HC * s + hc + 1)
                        nc.vector.tensor_tensor(h_lo[p][hc][:, :], h_s[:, hc, :], h_hi[p][hc][:, :].bitcast(F32),
                                                ALU.subtract).then_inc(hlo_ready, 1)
                        if hc == 1 and runs(t, c, -1, SLOTS):
                            x_low(t, c + 1)
                if runs(t, c, 0, SLOTS):
                    s, r = num(t, c), c % 4
                    dve.wait_ge(powers_ready, s + 1)
                    nc.vector.tensor_scalar(denom[:, :], powers[:, r, :, 0], 1.0, None, ALU.add).then_inc(denom_ready, 1)
                    dve.wait_ge(denom_ready, s + 1)
                    nc.vector.reciprocal(inverse[:, :], denom[:, :]).then_inc(inverse_ready, 1)
                    dve.wait_ge(inverse_ready, s + 1)
                    at_least(dve, y_weighted, s - 3)
                    nc.vector.tensor_tensor(weight[:, r, :], inverse[:, :], powers[:, r, :, 1], ALU.mult).then_inc(weight_ready, 1)

            x_low(0, 0)
            run_b(dve, step_b)

        @block.tensor
        def _(pe):
            pe.wait_ge(params_loaded, 16 * N_PARAMS)
            pe.wait_ge(pool_step, 8)
            pe.wait_ge(bias_ready, 1)

            def blk(bank_, b):
                return bank_[:, b * P:(b + 1) * P]

            def step(t, c):
                if runs(t, c, 3, GROUPS):
                    g, p, r = num(t, c - 3), (c - 3) % 2, (c - 3) % 4
                    pe.wait_ge(mask_ready, g + 1)
                    pe.wait_ge(seen_ready, g + 1)
                    at_least(pe, place_ready, g)
                    rank = ps_rank[:, 0:GB * E].rearrange("p (b e) -> p b e", b=GB)
                    nc.tensor.matmul(rank, before_bf[:, :], mask[:, p, :, :], start=True, stop=False)
                    for b in range(GB - 1):
                        nc.tensor.matmul(rank[:, b + 1:GB, :], ones_bf[:, :],
                                         mask[:, p, b, :].unsqueeze(1).to_broadcast([P, GB - 1 - b, E]), start=False, stop=False)
                    nc.tensor.matmul(rank, ones_bf[:, :], seen[:, r, :].unsqueeze(1).to_broadcast([P, GB, E]),
                                     start=False, stop=True).then_inc(rank_done, 1)
                if runs(t, c, 0, GROUPS):
                    g, p = num(t, c), c % 2
                    pe.wait_ge(n_ready, g + 1)
                    at_least(pe, hT_ready, g)
                    for b in range(GB):
                        last = nc.tensor.transpose(blk(ps_nT, b), n_s[:, p, b, :], ident[:, :])
                    last.then_inc(nT_done, 1)
                    pe.wait_ge(adj_loaded[p], 16 * uses(t, c, 2))
                    at_least(pe, adjT_ready, g)
                    for b in range(GB):
                        last = nc.tensor.transpose(blk(ps_adjT, b), adj_in[:, p, b, :], ident[:, :])
                    last.then_inc(adjT_done, 1)
                if runs(t, c, 0, GROUPS):
                    g, p = num(t, c), c % 2
                    pe.wait_ge(hT_ready, g + 1)
                    at_least(pe, rel_ready, g)
                    for b in range(GB):
                        last = nc.tensor.matmul(blk(ps_rel, b), hT[:, p, b, :], w_rel_s[:, :], start=True, stop=True)
                    last.then_inc(rel_done, 1)
                    at_least(pe, x1_ready, g)
                    nc.tensor.matmul(ps_conv[:, :], ones_bf[:, :], b_rel3[:, :, :].rearrange("p b t -> p (b t)"), start=True, stop=False)
                    for b in range(GB):
                        nc.tensor.matmul(blk(ps_conv, b), hT[:, p, b, :], w_root_s[:, :], start=False, stop=False)
                if runs(t, c, 2, GROUPS):
                    g, p = num(t, c - 2), (c - 2) % 2
                    pe.wait_ge(yT_ready, g + 1)
                    at_least(pe, score_ready, g)
                    for b in range(GB):
                        last = nc.tensor.matmul(blk(ps_gate, b), yT[:, p, b, :], w_gate_s[:, :], start=True, stop=True)
                    last.then_inc(gate_done, 1)
                if runs(t, c, 0, GROUPS):
                    g, p = num(t, c), c % 2
                    pe.wait_ge(rel_ready, g + 1)
                    pe.wait_ge(adjT_ready, g + 1)
                    for b in range(GB):
                        last = nc.tensor.matmul(blk(ps_conv, b), adjT[:, p, b, :], rel_s[:, p, b, :], start=False, stop=b == GB - 1)
                    last.then_inc(conv_done, 1)
                if runs(t, c, 1, GROUPS):
                    g, r = num(t, c - 1), (c - 1) % 4
                    pe.wait_ge(y_ready, g + 1)
                    at_least(pe, yT_ready, g)
                    for b in range(GB):
                        last = nc.tensor.transpose(blk(ps_yT, b), rows_s[:, r, 0, b, 0:P], ident[:, :])
                    last.then_inc(yT_done, 1)

            run_a(pe, step)

            pe.wait_ge(seen_ready, GROUPS + 1)
            pe.wait_ge(place_ready, GROUPS)
            nc.tensor.matmul(ps_rank[:, 0:E], ones_bf[:, :], seen[:, GROUPS % 4, :], start=True, stop=True).then_inc(lengths_done, 1)

            def x_turn(t, c):
                s, r = num(t, c), c % 4
                pe.wait_ge(xin_loaded[r], 16 * uses(t, c, 4))
                at_least(pe, xlo_ready, s)
                for j in range(SB):
                    last = nc.tensor.transpose(blk(ps_xT, j), xin[:, r, j, 0:P], ident[:, :])
                last.then_inc(xT_done, 1)

            def step_b(t, c):
                if runs(t, c, 0, SLOTS):
                    s, p = num(t, c), c % 2
                    pe.wait_ge(xlo_ready, s + 1)
                    pe.wait_ge(w1_loaded[p], 16 * uses(t, c, 2))
                    for hc in range(HC):
                        at_least(pe, h_ready, HC * (s - 1) + hc + 1)
                        high = w1_s[p][:, hc * P:(hc + 1) * P]
                        low = w1_s[p][:, H + hc * P:H + (hc + 1) * P]
                        nc.tensor.matmul(ps_h[hc][:, :], high, x_hi[p][:, :], start=True, stop=False)
                        nc.tensor.matmul(ps_h[hc][:, :], high, x_lo[p][:, :], start=False, stop=False)
                        nc.tensor.matmul(ps_h[hc][:, :], low, x_hi[p][:, :], start=False, stop=True).then_inc(h_done, 1)
                if runs(t, c, 2, SLOTS):
                    s, p = num(t, c - 2), (c - 2) % 2
                    pe.wait_ge(yslotT_ready, s + 1)
                    at_least(pe, y_weighted, s)
                    for j in range(SB):
                        last = nc.tensor.transpose(blk(ps_back, j), yT_s[:, p, j * P:(j + 1) * P], ident[:, :])
                    last.then_inc(back_done, 1)
                if runs(t, c, -1, SLOTS):
                    x_turn(t, c + 1)
                if runs(t, c, 1, SLOTS):
                    s, p = num(t, c - 1), (c - 1) % 2
                    pe.wait_ge(w2_loaded[p], 16 * uses(t, c - 1, 2))
                    at_least(pe, yslotT_ready, s)
                    for hc in range(HC):
                        pe.wait_ge(hlo_ready, HC * s + hc + 1)
                        high = w2_s[p][:, hc * P:(hc + 1) * P]
                        low = w2_s[p][:, H + hc * P:H + (hc + 1) * P]
                        nc.tensor.matmul(ps_y[:, :], high, h_hi[p][hc][:, :], start=hc == 0, stop=False)
                        nc.tensor.matmul(ps_y[:, :], high, h_lo[p][hc][:, :], start=False, stop=False)
                        last = nc.tensor.matmul(ps_y[:, :], low, h_hi[p][hc][:, :], start=False, stop=hc == HC - 1)
                    last.then_inc(yslot_done, 1)

            x_turn(0, 0)
            run_b(pe, step_b)


def kernel(x, adj, L0_gnn_W_rel, L0_gnn_b_rel, L0_gnn_W_root, L0_gnn_ln_gamma, L0_gnn_ln_beta,
           L0_ffn_Wg, L0_ffn_bg, L0_ffn_W1, L0_ffn_b1, L0_ffn_W2, L0_ffn_b2):
    import numpy as np
    import concourse.bacc as bacc
    from concourse.bass_utils import run_bass_kernel_spmd

    graphs, nodes, d = x.shape
    n_exp, hidden, _ = L0_ffn_W1.shape
    chunks = hidden // 128
    laid = {
        "x": x,
        "adj": adj,
        "w_rel": L0_gnn_W_rel,
        "b_rel": L0_gnn_b_rel,
        "w_root": L0_gnn_W_root,
        "gamma": np.reshape(L0_gnn_ln_gamma, (d, 1)),
        "beta": np.reshape(L0_gnn_ln_beta, (d, 1)),
        "w_gate": np.transpose(L0_ffn_Wg),
        "b_gate": L0_ffn_bg,
        "w1": np.transpose(L0_ffn_W1, (0, 2, 1)),
        "b1": np.transpose(np.reshape(L0_ffn_b1, (n_exp, chunks, 128)), (0, 2, 1)),
        "w2": np.reshape(np.transpose(np.reshape(L0_ffn_W2, (n_exp, d, chunks, 128)), (0, 3, 2, 1)), (n_exp, 128, hidden)),
        "b2": np.reshape(L0_ffn_b2, (n_exp, d, 1)),
    }
    nc = bacc.Bacc("TRN2", target_bir_lowering=False, num_devices=1)
    arrays, args = {}, []
    for name, a in laid.items():
        a = np.ascontiguousarray(a)
        arrays[f"in_{name}"] = a
        args.append(nc.dram_tensor(f"in_{name}", a.shape, mybir.dt.from_np(a.dtype), kind="ExternalInput").ap())
    tokens = graphs * nodes
    out = nc.dram_tensor("out_rows", [tokens + SPARE, d], F32, kind="ExternalOutput").ap()
    build_gnn_moe(nc, *args, out)
    r = run_bass_kernel_spmd(nc, [arrays], core_ids=[0])
    return np.reshape(r.results[0]["out_rows"][:tokens], (graphs, nodes, d))
```

```python
from contextlib import ExitStack

import concourse.bass as bass
from concourse import mybir

F32 = mybir.dt.float32
F32R = mybir.dt.float32r
BF16 = mybir.dt.bfloat16
I32 = mybir.dt.int32
U32 = mybir.dt.uint32
ALU = mybir.AluOpType
ACT = mybir.ActivationFunctionType
X = mybir.AxisListType.X

EPS = 1e-5
SPARE = 512


def build_gnn_moe(nc, x, adj, w_rel, b_rel, w_root, gamma, beta, w_gate, b_gate, w1, b1, w2, b2, out):
    P = 128
    GRAPHS = x.shape[0]
    T = GRAPHS * P
    GB = 4
    GROUPS = GRAPHS // GB
    E = w_gate.shape[1]
    TOP = 2
    H = w1.shape[2]
    HC = H // P
    SLOT = 512
    SB = SLOT // P
    SLOTS = TOP * T // SLOT + E - 1
    CAP = T + SLOT
    ROWS = E * CAP + SLOT
    META_ID, META_GAP, META_FIRST = P, P + 1, P + 2
    ROW = P + 3
    W1C, W2C = 2 * H + HC, 2 * H + 1
    TILES = T // SLOT

    routed = nc.dram_tensor("routed_rows", [ROWS, ROW], F32).ap()
    w1_split = nc.dram_tensor("w1_split", [E, P, W1C], F32).ap()
    w2_split = nc.dram_tensor("w2_split", [E, P, W2C], F32).ap()

    x_g = x.rearrange("(g b) t d -> g t b d", b=GB)
    adj_g = adj.rearrange("(g b) i j -> g i b j", b=GB)
    out_g = out[0:T, :].rearrange("(g b t) d -> g t b d", b=GB, t=P)

    with ExitStack() as ctx:
        def sb(name, shape, dt=F32):
            return ctx.enter_context(nc.sbuf_tensor(name, shape, dt))

        def sem(name):
            return ctx.enter_context(nc.semaphore(name))

        bank = [ctx.enter_context(nc.psum_tensor(f"bank{i}", [P, 512], F32)) for i in range(8)]
        ps_nT, ps_adjT, ps_rel, ps_conv, ps_yT, ps_gate, ps_rank = (bank[i] for i in range(7))
        ps_conv = [ps_conv, bank[7]]
        ps_h = bank[0:4]
        ps_xT, ps_y, ps_back = bank[4], bank[5], bank[6]

        ident = sb("ident", [P, P])
        ones_bf = sb("ones_bf", [P, P], BF16)
        before_bf = sb("before_bf", [P, P], BF16)
        w_rel_s = sb("w_rel_s", [P, P])
        w_root_s = sb("w_root_s", [P, P])
        gamma_s = sb("gamma_s", [P, 1])
        beta_s = sb("beta_s", [P, 1])
        w_gate_s = sb("w_gate_s", [P, P])
        b_gate_s = sb("b_gate_s", [P, E])
        b_rel_s = sb("b_rel_s", [P, P])
        b_part = sb("b_part", [P, 3, P], BF16)
        b_row = sb("b_row", [P, 3, P], BF16)
        b_rest = sb("b_rest", [P, 2, P])
        b_sum = sb("b_sum", [P, P], BF16)
        b_rel3 = sb("b_rel3", [P, GB, P], BF16)
        count_i = sb("count_i", [P, P], I32)
        expert_f = sb("expert_f", [P, E])
        base_f = sb("base_f", [P, E])
        tile_f = sb("tile_f", [P, TILES])
        slot_f = sb("slot_f", [P, SLOTS])
        order_f = sb("order_f", [P, E, E])
        ids = sb("ids", [P, GRAPHS], I32)
        fill = sb("fill", [P, SB, ROW])
        fill_id = sb("fill_id", [P, SB], I32)

        x_in = sb("x_in", [P, 2, GB, P])
        adj_in = sb("adj_in", [P, 2, GB, P])
        xstat = sb("xstat", [P, GB, 6])
        xmv = sb("xmv", [P, GB, 2])
        xvar = sb("xvar", [P, 2, GB])
        xroot = sb("xroot", [P, 2, GB])
        xr = sb("xr", [P, 2, GB])
        xscale = sb("xscale", [P, 2, GB])
        n_s = sb("n_s", [P, 2, GB, P])
        xl_s = sb("xl_s", [P, 2, GB, P])
        hT = sb("hT", [P, 2, GB, P])
        adjT = sb("adjT", [P, 2, GB, P])
        rel_s = sb("rel_s", [P, 2, GB, P])
        x1_s = sb("x1_s", [P, 2, GB, P])
        ystat = sb("ystat", [P, GB, 6])
        ymv = sb("ymv", [P, GB, 2])
        yvar = sb("yvar", [P, GB])
        yroot = sb("yroot", [P, GB])
        yr = sb("yr", [P, GB])
        yshift = sb("yshift", [P, GB])
        rows_s = sb("rows_s", [P, 4, GB, ROW])
        yT = sb("yT", [P, 2, GB, P])
        score = sb("score", [P, GB, E])
        top8 = sb("top8", [P, GB, 8])
        which = sb("which", [P, GB, 8], U32)
        which_f = sb("which_f", [P, 2, GB, TOP])
        gap = sb("gap", [P, 2, GB])
        hot = sb("hot", [P, 2, GB, TOP, E])
        mask = sb("mask", [P, 2, GB, E], BF16)
        seen = sb("seen", [P, 4, E], BF16)
        seen_add = sb("seen_add", [P, E])
        place = sb("place", [P, GB, E])
        placed = sb("placed", [P, GB, TOP, E])
        place_f = sb("place_f", [P, GB, TOP])
        place_i = sb("place_i", [P, 4, GB, TOP], I32)

        w_raw = sb("w_raw", [P, 2, E, H])
        b1_raw = sb("b1_raw", [P, E, HC])
        b2_raw = sb("b2_raw", [P, E, 1])
        w1_sp = sb("w1_sp", [P, W1C])
        w2_sp = sb("w2_sp", [P, W2C])

        length = sb("length", [P, E])
        over = sb("over", [P, E, TILES])
        tiles = sb("tiles", [P, E])
        upto = sb("upto", [P, E])
        tri_t = sb("tri_t", [P, E, E])
        past = sb("past", [P, SLOTS, E])
        pasted = sb("pasted", [P, SLOTS, E])
        s_exp = sb("s_exp", [P, SLOTS])
        s_start = sb("s_start", [P, SLOTS])
        s_row = sb("s_row", [P, SLOTS])
        s_live = sb("s_live", [P, SLOTS])
        s_new = sb("s_new", [P, SLOTS])
        ends_f = sb("ends_f", [P, E])
        ends = sb("ends", [P, E], I32)
        table = sb("table", [P, SLOTS + 2, 8], I32)

        xin = sb("xin", [P, 4, SB, ROW])
        w1_s = [sb(f"w1_s{i}", [P, W1C], F32R) for i in range(2)]
        w2_s = [sb(f"w2_s{i}", [P, W2C], F32R) for i in range(2)]
        x_hi = [sb(f"x_hi{i}", [P, SLOT], F32R) for i in range(2)]
        x_lo = [sb(f"x_lo{i}", [P, SLOT], F32R) for i in range(2)]
        h_s = sb("h_s", [P, HC, SLOT])
        h_hi = [[sb(f"h_hi{i}{c}", [P, SLOT], F32R) for c in range(HC)] for i in range(2)]
        h_lo = [[sb(f"h_lo{i}{c}", [P, SLOT], F32R) for c in range(HC)] for i in range(2)]
        yT_s = sb("yT_s", [P, 2, SLOT])
        y_s = sb("y_s", [P, 2, SB, P])
        row_id = sb("row_id", [P, 4, SB], I32)
        gaps = sb("gaps", [P, 4, SB, 2])
        powers = sb("powers", [P, 4, SB, 2])
        denom = sb("denom", [P, SB])
        inverse = sb("inverse", [P, SB])
        weight = sb("weight", [P, 4, SB])

        params_loaded = sem("params_loaded")
        b_rel_loaded = sem("b_rel_loaded")
        waits_passed = sem("waits_passed")
        pool_step = sem("pool_step")
        consts_ready = sem("consts_ready")
        split_ready = sem("split_ready")
        bias_ready = sem("bias_ready")
        rows_picked = sem("rows_picked")
        dve_step = sem("dve_step")
        raw_loaded = sem("raw_loaded")
        w_high = sem("w_high")
        w_split = sem("w_split")
        w_stored = sem("w_stored")
        x_loaded = [sem(f"x_loaded{i}") for i in range(2)]
        adj_loaded = [sem(f"adj_loaded{i}") for i in range(2)]
        xstat_done = sem("xstat_done")
        xmv_done = sem("xmv_done")
        xvar_done = sem("xvar_done")
        xroot_done = sem("xroot_done")
        xinv_done = sem("xinv_done")
        xscale_done = sem("xscale_done")
        n_ready = sem("n_ready")
        xl_ready = sem("xl_ready")
        nT_done = sem("nT_done")
        adjT_done = sem("adjT_done")
        hT_ready = sem("hT_ready")
        adjT_ready = sem("adjT_ready")
        rel_done = sem("rel_done")
        rel_ready = sem("rel_ready")
        conv_done = sem("conv_done")
        x1_ready = sem("x1_ready")
        x1_stored = [sem(f"x1_stored{i}") for i in range(2)]
        ystat_done = sem("ystat_done")
        ymv_done = sem("ymv_done")
        yvar_done = sem("yvar_done")
        yroot_done = sem("yroot_done")
        yinv_done = sem("yinv_done")
        yscale_done = sem("yscale_done")
        y_ready = sem("y_ready")
        yT_done = sem("yT_done")
        yT_ready = sem("yT_ready")
        gate_done = sem("gate_done")
        score_ready = sem("score_ready")
        top_ready = sem("top_ready")
        gap_ready = sem("gap_ready")
        which_ready = sem("which_ready")
        hot_ready = sem("hot_ready")
        mask_ready = sem("mask_ready")
        added_ready = sem("added_ready")
        seen_ready = sem("seen_ready")
        rank_done = sem("rank_done")
        place_ready = sem("place_ready")
        placed_ready = sem("placed_ready")
        placef_ready = sem("placef_ready")
        meta_ready = sem("meta_ready")
        scattered = [sem(f"scattered{i}") for i in range(4)]
        lengths_done = sem("lengths_done")
        ends_ready = sem("ends_ready")
        table_ready = sem("table_ready")
        fill_stored = sem("fill_stored")

        xin_loaded = [sem(f"xin_loaded{i}") for i in range(4)]
        w1_loaded = [sem(f"w1_loaded{i}") for i in range(2)]
        w2_loaded = [sem(f"w2_loaded{i}") for i in range(2)]
        xT_done = sem("xT_done")
        xhi_ready = sem("xhi_ready")
        xlo_ready = sem("xlo_ready")
        gaps_ready = sem("gaps_ready")
        powers_ready = sem("powers_ready")
        denom_ready = sem("denom_ready")
        inverse_ready = sem("inverse_ready")
        weight_ready = sem("weight_ready")
        h_done = sem("h_done")
        h_ready = sem("h_ready")
        hhi_ready = sem("hhi_ready")
        hlo_ready = sem("hlo_ready")
        yslot_done = sem("yslot_done")
        yslotT_ready = sem("yslotT_ready")
        back_done = sem("back_done")
        y_weighted = sem("y_weighted")
        added = [sem(f"added{i}") for i in range(2)]

        N_PARAMS = 6

        def at_least(eng, s, value):
            if isinstance(value, int) and value <= 0:
                return
            eng.wait_ge(s, value)

        def apart(eng):
            eng.sem_inc(waits_passed, 1)

        def num(t, c):
            return 4 * t + c

        def uses(t, c, ring):
            return t * (4 // ring) + c // ring + 1

        def pipeline(eng, step, first_full, n, lag_end):
            rounds = (n - first_full) // 4
            for i in range(first_full):
                step(0, i)
            with eng.Fori(0, rounds) as t:
                for c in range(4):
                    step(t, first_full + c)
            for i in range(first_full + 4 * rounds, n + lag_end):
                step(0, i)

        def runs(t, c, lag, n):
            i = 4 * t + c if isinstance(t, int) else None
            return i is None or 0 <= i - lag < n

        A_FULL, A_LAG = 5, 3
        B_FULL, B_LAG = 4, 2
        B_LAST = SLOTS - 1

        def run_a(eng, step):
            pipeline(eng, step, A_FULL, GROUPS - 1, 1 + A_LAG)

        def run_b(eng, step):
            pipeline(eng, step, B_FULL, B_LAST, 1 + B_LAG)

        block = ctx.enter_context(nc.Block())

        @block.sync
        def _(sp):
            def load(t, c):
                g, p = num(t, c), c % 2
                at_least(sp, xl_ready, g - 1)
                at_least(sp, n_ready, g - 1)
                sp.dma_start(x_in[:, p, :, :], x_g[g]).then_inc(x_loaded[p], 16)
                at_least(sp, adjT_done, g - 1)
                sp.dma_start(adj_in[:, p, :, :], adj_g[g]).then_inc(adj_loaded[p], 16)

            def store(t, c):
                g, p = num(t, c), c % 2
                sp.wait_ge(x1_ready, g + 1)
                sp.dma_start(out_g[g], x1_s[:, p, :, :]).then_inc(x1_stored[p], 16)

            def load_params(*pairs):
                for dst, src in pairs:
                    sp.dma_start(dst, src).then_inc(params_loaded, 16)

            sp.dma_start(x_in[:, 0, :, :], x_g[0]).then_inc(x_loaded[0], 16)
            sp.dma_start(b_rel_s[:, :], b_rel.partition_broadcast(P)).then_inc(b_rel_loaded, 16)
            load_params((gamma_s[:, :], gamma), (beta_s[:, :], beta), (w_rel_s[:, :], w_rel), (w_root_s[:, :], w_root))
            sp.dma_start(adj_in[:, 0, :, :], adj_g[0]).then_inc(adj_loaded[0], 16)
            load_params((b_gate_s[:, :], b_gate.partition_broadcast(P)))
            sp.wait_ge(consts_ready, 1)
            sp.dma_start(w_gate_s[:, 0:E], w_gate).then_inc(params_loaded, 16)

            def store_weights(e):
                sp.wait_ge(w_split, e + 1)
                for both, split in ((w1_sp, w1_split), (w2_sp, w2_split)):
                    dst = split[e] if isinstance(e, int) else split[bass.ds(e, 1)].rearrange("a p c -> p (a c)")
                    sp.dma_start(dst, both[:, :]).then_inc(w_stored, 16)

            def step(t, c):
                if runs(t, c, -1, GROUPS):
                    load(t, c + 1)
                if runs(t, c, 1, GROUPS):
                    store(t, c - 1)
                if not isinstance(t, int) and c == 6:
                    store_weights(t)

            pipeline(sp, step, 3, GROUPS - 1, 2)
            store_weights(E - 1)

            sp.wait_ge(ends_ready, 1)
            BOUNDED = "part P's arithmetic keeps each value in the bounds that the shapes give"
            _, list_ends = nc.values_load_multi_w_load_instructions(
                ends[0:1, :], engines=[mybir.EngineType.SP], min_val=0, max_val=ROWS - SLOT, skip_runtime_bounds_check_because=BOUNDED)
            for end in list_ends:
                dst = routed[bass.ds(end, SLOT), :].rearrange("(j p) d -> p j d", p=P)
                sp.dma_start(dst, fill[:, :, :]).then_inc(fill_stored, 16)
            sp.dma_start(routed[E * CAP:ROWS, :].rearrange("(j p) d -> p j d", p=P),
                         fill[:, :, :]).then_inc(fill_stored, 16)
            sp.dma_start(out[T:T + SPARE, :].rearrange("(j p) d -> p j d", p=P),
                         fill[:, :, 0:P]).then_inc(fill_stored, 16)
            sp.wait_ge(fill_stored, 16 * (E + 2))
            for r in range(4):
                sp.wait_ge(scattered[r], 128 * (GROUPS // 4))
            sp.wait_ge(w_stored, 32 * E)
            for p in range(2):
                sp.wait_ge(x1_stored[p], 16 * (GROUPS // 2))

            sp.wait_ge(table_ready, 1)

            def step_b(t, c):
                s = num(t, c)
                at = slice(s + 2, s + 3) if isinstance(s, int) else bass.ds(s + 2, 1)
                _, (row, e1, new1, e2, new2) = nc.values_load_multi_w_load_instructions(
                    table[0:1, at, 0:5].rearrange("p a c -> p (a c)"), engines=[mybir.EngineType.SP], min_val=0, max_val=ROWS - SLOT,
                    skip_runtime_bounds_check_because=BOUNDED)
                e1, e2 = (nc.s_assert_within(e, 0, E - 1, skip_runtime_bounds_check_because=BOUNDED) for e in (e1, e2))
                new1, new2 = (nc.s_assert_within(n, 0, 1, skip_runtime_bounds_check_because=BOUNDED) for n in (new1, new2))
                if runs(t, c, -2, SLOTS):
                    r = (c + 2) % 4
                    at_least(sp, xT_done, s - 1)
                    at_least(sp, gaps_ready, s - 1)
                    src = routed[bass.ds(row, SLOT), :].rearrange("(j p) d -> p j d", p=P)
                    sp.dma_start(xin[:, r, :, :], src).then_inc(xin_loaded[r], 16)
                if runs(t, c, -1, SLOTS):
                    p = (c + 1) % 2
                    at_least(sp, h_ready, HC * s)
                    sp.dma_start(w1_s[p][:, :].bitcast(F32), w1_split[bass.ds(e1, 1), :, :].rearrange("a p c -> p (a c)"),
                                 cond=new1).then_inc(w1_loaded[p], 16)
                if runs(t, c, 0, SLOTS):
                    p = c % 2
                    at_least(sp, yslotT_ready, s - 1)
                    sp.dma_start(w2_s[p][:, :].bitcast(F32), w2_split[bass.ds(e2, 1), :, :].rearrange("a p c -> p (a c)"),
                                 cond=new2).then_inc(w2_loaded[p], 16)

            step_b(0, -2)
            step_b(0, -1)
            pipeline(sp, step_b, 3, SLOTS - 2, 2)
            sp.wait_ge(added[0], 64 * ((SLOTS + 1) // 2))
            sp.wait_ge(added[1], 64 * (SLOTS // 2))

        @block.gpsimd
        def _(pool):
            nc.gpsimd.memset(w_gate_s[:, :], 0.0).then_inc(consts_ready, 1)
            nc.gpsimd.memset(ident[:, :], 0.0).then_inc(pool_step, 1)
            nc.gpsimd.memset(ones_bf[:, :], 1.0).then_inc(pool_step, 1)
            nc.gpsimd.memset(fill[:, :, :], 0.0).then_inc(pool_step, 1)
            pool.wait_ge(pool_step, 3)
            nc.gpsimd.affine_select(out=ident[:, :], in_=ident[:, :], compare_op=ALU.not_equal, fill=1.0,
                                    base=0, pattern=[[-1, P]], channel_multiplier=1).then_inc(pool_step, 1)
            nc.gpsimd.affine_select(out=before_bf[:, :], in_=ones_bf[:, :], compare_op=ALU.is_gt, fill=0.0,
                                    base=0, pattern=[[1, P]], channel_multiplier=-1).then_inc(pool_step, 1)
            nc.gpsimd.iota(ids[:, :], pattern=[[P, GRAPHS]], base=0, channel_multiplier=1).then_inc(pool_step, 1)
            nc.gpsimd.iota(fill_id[:, :], pattern=[[P, SB]], base=T, channel_multiplier=1).then_inc(pool_step, 1)
            pool.wait_ge(pool_step, 7)
            nc.gpsimd.tensor_copy(fill[:, :, META_ID:META_ID + 1].bitcast(I32),
                                  fill_id[:, :].unsqueeze(2)).then_inc(pool_step, 1)
            made = 8
            for dst, n, pattern in ((expert_f[:, :], E, [[1, E]]), (base_f[:, :], E, [[CAP, E]]),
                                    (tile_f[:, :], TILES, [[SLOT, TILES]]), (slot_f[:, :], SLOTS, [[1, SLOTS]]),
                                    (order_f[:, :, :].rearrange("p e f -> p (e f)"), E * E, [[1, E], [-1, E]])):
                nc.gpsimd.iota(count_i[:, 0:n], pattern=pattern, base=0, channel_multiplier=0).then_inc(pool_step, 1)
                made += 1
                pool.wait_ge(pool_step, made)
                nc.gpsimd.tensor_copy(dst, count_i[:, 0:n]).then_inc(pool_step, 1)
                made += 1
                pool.wait_ge(pool_step, made)
            pool.wait_ge(split_ready, 1)
            for k in range(3):
                nc.gpsimd.affine_select(out=b_row[:, k, :], in_=b_part[:, k, :], compare_op=ALU.is_equal, fill=0.0,
                                        base=-k, pattern=[[0, P]], channel_multiplier=1).then_inc(rows_picked, 1)

            def step(t, c):
                if runs(t, c, 3, GROUPS):
                    g, r = num(t, c - 3), (c - 3) % 4
                    pool.wait_ge(meta_ready, g + 1)
                    apart(pool)
                    for b in range(GB):
                        for k in range(TOP):
                            pool.indirect_dma_start(
                                out=routed, out_offset=bass.IndirectOffsetOnAxis(ap=place_i[:, r, b, k:k + 1], axis=0),
                                in_=rows_s[:, r, b, :], in_offset=None).then_inc(scattered[r], 16)

            run_a(pool, step)

            def step_b(t, c):
                if runs(t, c, 2, SLOTS):
                    s, p, r = num(t, c - 2), (c - 2) % 2, (c - 2) % 4
                    pool.wait_ge(y_weighted, s + 1)
                    pool.wait_ge(gaps_ready, s + 1)
                    at_least(pool, added[1 - p], 64 * uses(t, c - 3, 2) if c >= 3 or not isinstance(t, int) else 0)
                    apart(pool)
                    for j in range(SB):
                        pool.indirect_dma_start(
                            out=out, out_offset=bass.IndirectOffsetOnAxis(
                                ap=row_id[:, r, j:j + 1], axis=0),
                            in_=y_s[:, p, j, :], in_offset=None, compute_op=ALU.add,
                            bounds_check=T + SPARE - 1).then_inc(added[p], 16)

            run_b(pool, step_b)

        @block.scalar
        def _(act):
            def load_weights():
                for e in range(E):
                    for n, w in enumerate((w1, w2)):
                        act.dma_start(w_raw[:, n, e, :], w[e]).then_inc(raw_loaded, 16)
                act.dma_start(b1_raw[:, :, :], b1).then_inc(raw_loaded, 16)
                act.dma_start(b2_raw[:, :, 0], b2).then_inc(raw_loaded, 16)

            def x_root(t, c):
                act.wait_ge(xvar_done, num(t, c) + 1)
                nc.scalar.activation(xroot[:, :, :], xvar[:, :, :], ACT.Sqrt).then_inc(xroot_done, 1)

            def step(t, c):
                if runs(t, c, 0, GROUPS):
                    g, p = num(t, c), c % 2
                    act.wait_ge(nT_done, g + 1)
                    at_least(act, rel_done, g - 1)
                    at_least(act, conv_done, g - 1)
                    nc.scalar.activation(hT[:, p, :, :], ps_nT[:, :].rearrange("p (b t) -> p b t", b=GB),
                                         ACT.Identity, bias=beta_s[:, 0:1], scale=gamma_s[:, 0:1]).then_inc(hT_ready, 1)
                if runs(t, c, 2, GROUPS):
                    g, p = num(t, c - 2), (c - 2) % 2
                    act.wait_ge(yT_done, g + 1)
                    at_least(act, gate_done, g - 1)
                    nc.scalar.activation(yT[:, p, :, :], ps_yT[:, :].rearrange("p (b t) -> p b t", b=GB),
                                         ACT.Copy).then_inc(yT_ready, 1)
                if runs(t, c, 0, GROUPS):
                    g, p = num(t, c), c % 2
                    act.wait_ge(adjT_done, g + 1)
                    nc.scalar.activation(adjT[:, p, :, :], ps_adjT[:, :].rearrange("p (b t) -> p b t", b=GB),
                                         ACT.Copy).then_inc(adjT_ready, 1)
                    act.wait_ge(rel_done, g + 1)
                    nc.scalar.activation(rel_s[:, p, :, :], ps_rel[:, :].rearrange("p (b t) -> p b t", b=GB),
                                         ACT.Copy).then_inc(rel_ready, 1)
                    act.wait_ge(xscale_done, g + 1)
                    act.wait_ge(x_loaded[p], 16 * uses(t, c, 2))
                    at_least(act, x1_ready, g - 1)
                    for b in range(GB):
                        last = nc.scalar.activation(xl_s[:, p, b, :], x_in[:, p, b, :], ACT.Identity,
                                                    bias=xscale[:, 1, b:b + 1], scale=xscale[:, 0, b:b + 1])
                    last.then_inc(xl_ready, 1)
                if runs(t, c, 1, GROUPS):
                    act.wait_ge(yvar_done, num(t, c - 1) + 1)
                    nc.scalar.activation(yroot[:, :], yvar[:, :], ACT.Sqrt).then_inc(yroot_done, 1)
                if runs(t, c, -1, GROUPS):
                    x_root(t, c + 1)
                if runs(t, c, 1, GROUPS):
                    g, p, r = num(t, c - 1), (c - 1) % 2, (c - 1) % 4
                    act.wait_ge(yscale_done, g + 1)
                    if not isinstance(g, int) or g >= 4:
                        at_least(act, scattered[r], 128 * (uses(t, c - 1, 4) - 1))
                    for b in range(GB):
                        last = nc.scalar.activation(rows_s[:, r, b, 0:P], x1_s[:, p, b, :], ACT.Identity,
                                                    bias=yshift[:, b:b + 1], scale=yr[:, b:b + 1])
                    last.then_inc(y_ready, 1)
                if isinstance(t, int) and c == 1:
                    load_weights()

            x_root(0, 0)
            act.wait_ge(params_loaded, 16 * N_PARAMS)
            run_a(act, step)

            def step_b(t, c):
                s = num(t, c)
                if runs(t, c, 0, SLOTS):
                    p = c % 2
                    for hc in range(HC):
                        act.wait_ge(h_done, HC * s + hc + 1)
                        at_least(act, hlo_ready, HC * (s - 1) + hc + 1)
                        nc.scalar.activation(h_s[:, hc, :], ps_h[hc][:, :], ACT.Relu,
                                             bias=w1_s[p][:, 2 * H + hc:2 * H + hc + 1].bitcast(F32)).then_inc(h_ready, 1)
                    x_powers(t, c)
                if runs(t, c, -1, SLOTS):
                    x_high(t, c + 1)
                if runs(t, c, 2, SLOTS):
                    s2, p, r = num(t, c - 2), (c - 2) % 2, (c - 2) % 4
                    act.wait_ge(back_done, s2 + 1)
                    act.wait_ge(weight_ready, s2 + 1)
                    if not isinstance(s2, int) or s2 >= 2:
                        at_least(act, added[p], 64 * (uses(t, c - 2, 2) - 1))
                    for j in range(SB):
                        last = nc.scalar.activation(y_s[:, p, j, :], ps_back[:, j * P:(j + 1) * P], ACT.Copy,
                                                    scale=weight[:, r, j:j + 1])
                    last.then_inc(y_weighted, 1)

            def x_high(t, c):
                s, p = num(t, c), c % 2
                act.wait_ge(xT_done, s + 1)
                at_least(act, h_done, HC * (s - 1))
                nc.scalar.activation(x_hi[p][:, :], ps_xT[:, :], ACT.Copy).then_inc(xhi_ready, 1)

            def x_powers(t, c):
                s, r = num(t, c), c % 4
                act.wait_ge(gaps_ready, s + 1)
                at_least(act, weight_ready, s - 3)
                nc.scalar.activation(powers[:, r, :, :], gaps[:, r, :, :], ACT.Exp).then_inc(powers_ready, 1)

            x_high(0, 0)
            run_b(act, step_b)

        @block.vector
        def _(dve):
            steps = [0]

            def link(ins):
                steps[0] += 1
                ins.then_inc(dve_step, 1)
                dve.wait_ge(dve_step, steps[0])

            def stage1_stats(t, c):
                g, p = num(t, c), c % 2
                dve.wait_ge(x_loaded[p], 16 * uses(t, c, 2))
                for b in range(GB):
                    last = nc.vector.bn_stats(xstat[:, b, :], x_in[:, p, b, :])
                last.then_inc(xstat_done, 1)

            def stage1_aggr(t, c):
                g = num(t, c)
                dve.wait_ge(xstat_done, g + 1)
                apart(dve)
                for b in range(GB):
                    last = nc.vector.bn_aggr(xmv[:, b, :], xstat[:, b, :])
                last.then_inc(xmv_done, 1)

            def stage1_var(t, c):
                g = num(t, c)
                dve.wait_ge(xmv_done, g + 1)
                at_least(dve, xroot_done, g)
                nc.vector.tensor_scalar(xvar[:, 0, :], xmv[:, :, 1], EPS, None, ALU.add)
                nc.vector.tensor_scalar(xvar[:, 1, :], xmv[:, :, 1], 1.0 + EPS, EPS * EPS, ALU.mult, ALU.add).then_inc(xvar_done, 1)

            def stage1(t, c):
                g, p = num(t, c), c % 2
                dve.wait_ge(xroot_done, g + 1)
                nc.vector.reciprocal(xr[:, :, :], xroot[:, :, :]).then_inc(xinv_done, 1)
                dve.wait_ge(xinv_done, g + 1)
                at_least(dve, xl_ready, g)
                nc.vector.tensor_scalar(xscale[:, 0, :], xr[:, 0, :], 1.0, None, ALU.add)
                nc.vector.scalar_tensor_tensor(out=xscale[:, 1, :], in0=xmv[:, :, 0], scalar=-1.0, in1=xr[:, 0, :],
                                               op0=ALU.mult, op1=ALU.mult).then_inc(xscale_done, 1)
                at_least(dve, nT_done, g - 1)
                for b in range(GB):
                    last = nc.vector.tensor_scalar(n_s[:, p, b, :], x_in[:, p, b, :], xmv[:, b, 0:1], xr[:, 1, b:b + 1],
                                                   ALU.subtract, ALU.mult)
                last.then_inc(n_ready, 1)

            def stage2_x1(t, c):
                g, p = num(t, c), c % 2
                dve.wait_ge(conv_done, g + 1)
                dve.wait_ge(xl_ready, g + 1)
                if not isinstance(g, int) or g >= 2:
                    at_least(dve, x1_stored[p], 16 * (uses(t, c, 2) - 1))
                at_least(dve, y_ready, g - 1)
                nc.vector.scalar_tensor_tensor(out=x1_s[:, p, :, :], in0=ps_conv[p][:, :].rearrange("p (b t) -> p b t", b=GB),
                                               scalar=0.0, in1=xl_s[:, p, :, :], op0=ALU.max, op1=ALU.add).then_inc(x1_ready, 1)

            def stage2_stats(t, c):
                g, p = num(t, c), c % 2
                dve.wait_ge(x1_ready, g + 1)
                for b in range(GB):
                    last = nc.vector.bn_stats(ystat[:, b, :], x1_s[:, p, b, :])
                last.then_inc(ystat_done, 1)

            def stage2_aggr(t, c):
                g = num(t, c)
                dve.wait_ge(ystat_done, g + 1)
                apart(dve)
                for b in range(GB):
                    last = nc.vector.bn_aggr(ymv[:, b, :], ystat[:, b, :])
                last.then_inc(ymv_done, 1)

            def stage2_var(t, c):
                dve.wait_ge(ymv_done, num(t, c) + 1)
                nc.vector.tensor_scalar(yvar[:, :], ymv[:, :, 1], EPS, None, ALU.add).then_inc(yvar_done, 1)

            def stage2_root(t, c):
                g = num(t, c)
                dve.wait_ge(yroot_done, g + 1)
                at_least(dve, y_ready, g)
                nc.vector.reciprocal(yr[:, :], yroot[:, :]).then_inc(yinv_done, 1)

            def stage2_shift(t, c):
                dve.wait_ge(yinv_done, num(t, c) + 1)
                nc.vector.scalar_tensor_tensor(out=yshift[:, :], in0=ymv[:, :, 0], scalar=-1.0, in1=yr[:, :],
                                               op0=ALU.mult, op1=ALU.mult).then_inc(yscale_done, 1)

            def stage3_score(t, c):
                g = num(t, c)
                dve.wait_ge(gate_done, g + 1)
                nc.vector.tensor_tensor(score[:, :, :], ps_gate[:, :].rearrange("p (b e) -> p b e", b=GB)[:, :, 0:E],
                                        b_gate_s[:, :].unsqueeze(1).to_broadcast([P, GB, E]), ALU.add).then_inc(score_ready, 1)

            def stage3_top(t, c):
                dve.wait_ge(score_ready, num(t, c) + 1)
                apart(dve)
                for b in range(GB):
                    last = nc.vector.max(top8[:, b, :], score[:, b, :])
                last.then_inc(top_ready, 1)

            def stage3_which(t, c):
                g, p = num(t, c), c % 2
                dve.wait_ge(top_ready, g + 1)
                apart(dve)
                for b in range(GB):
                    last = nc.vector.max_index(which[:, b, :], top8[:, b, :], score[:, b, :])
                last.then_inc(which_ready, 1)
                nc.vector.tensor_tensor(gap[:, p, :], top8[:, :, 1], top8[:, :, 0], ALU.subtract).then_inc(gap_ready, 1)

            def stage3_float(t, c):
                g, p = num(t, c), c % 2
                dve.wait_ge(which_ready, g + 1)
                nc.vector.tensor_copy(which_f[:, p, :, :], which[:, :, 0:TOP]).then_inc(hot_ready, 1)

            def stage3_hot(t, c):
                g, p = num(t, c), c % 2
                dve.wait_ge(hot_ready, 2 * g + 1)
                nc.vector.tensor_tensor(hot[:, p, :, :, :], which_f[:, p, :, :].unsqueeze(3).to_broadcast([P, GB, TOP, E]),
                                        expert_f[:, :].unsqueeze(1).unsqueeze(1).to_broadcast([P, GB, TOP, E]),
                                        ALU.is_equal).then_inc(hot_ready, 1)

            def stage3_mask(t, c):
                g, p = num(t, c), c % 2
                dve.wait_ge(hot_ready, 2 * g + 2)
                at_least(dve, rank_done, g - 1)
                nc.vector.tensor_tensor(mask[:, p, :, :], hot[:, p, :, 0, :], hot[:, p, :, 1, :], ALU.add).then_inc(mask_ready, 1)

            def stage3_add(t, c):
                g, p = num(t, c), c % 2
                dve.wait_ge(mask_ready, g + 1)
                nc.vector.tensor_reduce(seen_add[:, :], mask[:, p, :, :].rearrange("p b e -> p e b"), X, ALU.add).then_inc(added_ready, 1)

            def stage3_seen(t, c):
                g, r = num(t, c), c % 4
                dve.wait_ge(added_ready, g + 1)
                at_least(dve, rank_done, g - 2)
                nc.vector.tensor_tensor(seen[:, (r + 1) % 4, :], seen[:, r, :], seen_add[:, :], ALU.add).then_inc(seen_ready, 1)

            def stage4_place(t, c):
                dve.wait_ge(rank_done, num(t, c) + 1)
                nc.vector.tensor_tensor(place[:, :, :], ps_rank[:, 0:GB * E].rearrange("p (b e) -> p b e", b=GB),
                                        base_f[:, :].unsqueeze(1).to_broadcast([P, GB, E]), ALU.add).then_inc(place_ready, 1)

            def stage4_pick(t, c):
                g, p = num(t, c), c % 2
                dve.wait_ge(place_ready, g + 1)
                nc.vector.tensor_tensor(placed[:, :, :, :], hot[:, p, :, :, :],
                                        place[:, :, :].unsqueeze(2).to_broadcast([P, GB, TOP, E]), ALU.mult).then_inc(placed_ready, 1)

            def stage4_meta(t, c):
                g, p, r = num(t, c), c % 2, c % 4
                dve.wait_ge(gap_ready, g + 1)
                dve.wait_ge(y_ready, g + 1)
                nc.vector.tensor_copy(rows_s[:, r, :, META_GAP], gap[:, p, :])
                nc.vector.tensor_copy(rows_s[:, r, :, META_FIRST], which_f[:, p, :, 0])
                ids_g = ids[:, GB * g:GB * g + GB] if isinstance(g, int) else ids[:, bass.ds(GB * g, GB)]
                nc.vector.tensor_copy(rows_s[:, r, :, META_ID].bitcast(I32), ids_g)
                dve.wait_ge(placed_ready, g + 1)
                nc.vector.tensor_reduce(place_f[:, :, :], placed[:, :, :, :], X, ALU.add).then_inc(placef_ready, 1)

            def stage4_int(t, c):
                g, r = num(t, c), c % 4
                dve.wait_ge(placef_ready, g + 1)
                nc.vector.tensor_copy(place_i[:, r, :, :], place_f[:, :, :]).then_inc(meta_ready, 1)

            stage1_stats(0, 0)
            stage1_aggr(0, 0)
            stage1_var(0, 0)
            dve.wait_ge(b_rel_loaded, 16)
            link(nc.vector.tensor_copy(b_part[:, 0, :], b_rel_s[:, :]))
            link(nc.vector.tensor_tensor(b_rest[:, 0, :], b_rel_s[:, :], b_part[:, 0, :], ALU.subtract))
            link(nc.vector.tensor_copy(b_part[:, 1, :], b_rest[:, 0, :]))
            link(nc.vector.tensor_tensor(b_rest[:, 1, :], b_rest[:, 0, :], b_part[:, 1, :], ALU.subtract))
            nc.vector.tensor_copy(b_part[:, 2, :], b_rest[:, 1, :]).then_inc(split_ready, 1)
            nc.vector.memset(seen[:, 0, :], 0.0).then_inc(seen_ready, 1)
            dve.wait_ge(rows_picked, 3)
            link(nc.vector.tensor_tensor(b_sum[:, :], b_row[:, 0, :], b_row[:, 1, :], ALU.add))
            link(nc.vector.tensor_tensor(b_sum[:, :], b_sum[:, :], b_row[:, 2, :], ALU.add))
            nc.vector.tensor_copy(b_rel3[:, :, :], b_sum[:, :].unsqueeze(1).to_broadcast([P, GB, P])).then_inc(bias_ready, 1)

            dve.wait_ge(params_loaded, 16 * N_PARAMS)

            ORDER = ((stage1, 0), (stage4_place, 3), (stage2_x1, 1), (stage4_pick, 3), (stage2_stats, 1), (stage4_meta, 3),
                     (stage2_aggr, 1), (stage4_int, 3), (stage1_stats, -1), (stage2_var, 1), (stage1_aggr, -1),
                     (stage3_score, 2), (stage1_var, -1), (stage3_top, 2), (stage3_which, 2), (stage2_root, 1),
                     (stage3_float, 2), (stage2_shift, 1), (stage3_hot, 2), (stage3_mask, 2), (stage3_add, 2),
                     (stage3_seen, 2))

            def step(t, c):
                for part, lag in ORDER:
                    if runs(t, c, lag, GROUPS):
                        part(t, c - lag)
                if isinstance(t, int) and c == A_FULL - 1:
                    split_weights(0)
                if isinstance(t, int) and c == GROUPS - 1:
                    split_weights(E - 1)
                if not isinstance(t, int) and c == A_FULL + 3:
                    split_weights(t + 1)

            def split_weights(e):
                dve.wait_ge(raw_loaded, 16 * (2 * E + 2))
                at_least(dve, w_stored, 32 * e)
                halves = []
                for both, bias in ((w1_sp, b1_raw), (w2_sp, b2_raw)):
                    raw = bias[:, e, :] if isinstance(e, int) else bias[:, bass.ds(e, 1), :].rearrange("p a c -> p (a c)")
                    nc.vector.tensor_copy(both[:, 2 * H:], raw)
                for n, both in enumerate((w1_sp, w2_sp)):
                    one = e if isinstance(e, int) else bass.ds(e, 1)
                    raw = w_raw[:, n, one, :] if isinstance(e, int) else w_raw[:, n, one, :].rearrange("p a c -> p (a c)")
                    halves.append((both, raw))
                    nc.vector.tensor_copy(both[:, 0:H].bitcast(F32R), raw).then_inc(w_high, 1)
                dve.wait_ge(w_high, 2 * (e + 1))
                for both, raw in halves:
                    last = nc.vector.tensor_tensor(both[:, H:2 * H].bitcast(F32R), raw, both[:, 0:H], ALU.subtract)
                last.then_inc(w_split, 1)

            run_a(dve, step)

            dve.wait_ge(lengths_done, 1)
            link(nc.vector.tensor_copy(length[:, :], ps_rank[:, 0:E]))
            link(nc.vector.tensor_tensor(ends_f[:, :], length[:, :], base_f[:, :], ALU.add))
            nc.vector.tensor_copy(ends[:, :], ends_f[:, :]).then_inc(ends_ready, 1)
            link(nc.vector.tensor_tensor(over[:, :, :], length[:, :].unsqueeze(2).to_broadcast([P, E, TILES]),
                                         tile_f[:, :].unsqueeze(1).to_broadcast([P, E, TILES]), ALU.is_gt))
            link(nc.vector.tensor_reduce(tiles[:, :], over[:, :, :], X, ALU.add))
            link(nc.vector.tensor_scalar(tri_t[:, :, :], order_f[:, :, :], 0.0, None, ALU.is_ge))
            link(nc.vector.tensor_tensor(tri_t[:, :, :], tri_t[:, :, :], tiles[:, :].unsqueeze(1).to_broadcast([P, E, E]), ALU.mult))
            link(nc.vector.tensor_reduce(upto[:, :], tri_t[:, :, :], X, ALU.add))
            link(nc.vector.tensor_tensor(past[:, :, :], slot_f[:, :].unsqueeze(2).to_broadcast([P, SLOTS, E]),
                                         upto[:, :].unsqueeze(1).to_broadcast([P, SLOTS, E]), ALU.is_ge))
            link(nc.vector.tensor_reduce(s_exp[:, :], past[:, :, :], X, ALU.add))
            link(nc.vector.tensor_tensor(pasted[:, :, :], past[:, :, :], tiles[:, :].unsqueeze(1).to_broadcast([P, SLOTS, E]), ALU.mult))
            link(nc.vector.tensor_reduce(s_start[:, :], pasted[:, :, :], X, ALU.add))
            link(nc.vector.tensor_scalar(s_live[:, :], s_exp[:, :], float(E), float(SLOT), ALU.is_lt, ALU.mult))
            link(nc.vector.tensor_tensor(s_row[:, :], slot_f[:, :], s_start[:, :], ALU.subtract))
            link(nc.vector.tensor_tensor(s_row[:, :], s_row[:, :], s_live[:, :], ALU.mult))
            link(nc.vector.scalar_tensor_tensor(out=s_row[:, :], in0=s_exp[:, :], scalar=float(CAP), in1=s_row[:, :],
                                                op0=ALU.mult, op1=ALU.add))
            link(nc.vector.tensor_scalar(s_exp[:, :], s_exp[:, :], float(E - 1), None, ALU.min))
            nc.vector.memset(s_new[:, 0:2], 1.0)
            link(nc.vector.tensor_tensor(s_new[:, 2:SLOTS], s_exp[:, 2:SLOTS], s_exp[:, 0:SLOTS - 2], ALU.not_equal))
            link(nc.vector.memset(table[:, :, :], 0))
            nc.vector.tensor_copy(table[:, 0:SLOTS, 0], s_row[:, :])
            nc.vector.tensor_copy(table[:, 1:SLOTS + 1, 1], s_exp[:, :])
            nc.vector.tensor_copy(table[:, 1:SLOTS + 1, 2], s_new[:, :])
            nc.vector.tensor_copy(table[:, 2:SLOTS + 2, 3], s_exp[:, :])
            nc.vector.tensor_copy(table[:, 2:SLOTS + 2, 4], s_new[:, :]).then_inc(table_ready, 1)

            def x_low(t, c):
                s, p = num(t, c), c % 2
                dve.wait_ge(xhi_ready, s + 1)
                at_least(dve, h_done, HC * (s - 1))
                nc.vector.tensor_tensor(x_lo[p][:, :], ps_xT[:, :], x_hi[p][:, :].bitcast(F32), ALU.subtract).then_inc(xlo_ready, 1)
                r = c % 4
                dve.wait_ge(xin_loaded[r], 16 * uses(t, c, 4))
                if not isinstance(s, int) or s >= 4:
                    at_least(dve, added[p], 64 * (uses(t, c, 2) - 2))
                nc.vector.tensor_copy(row_id[:, r, :], xin[:, r, :, META_ID].bitcast(I32))
                nc.vector.tensor_copy(gaps[:, r, :, 0], xin[:, r, :, META_GAP])
                own = s_exp[:, s:s + 1] if isinstance(s, int) else s_exp[:, bass.ds(s, 1)]
                nc.vector.scalar_tensor_tensor(out=gaps[:, r, :, 1], in0=xin[:, r, :, META_FIRST], scalar=own, in1=xin[:, r, :, META_GAP],
                                               op0=ALU.not_equal, op1=ALU.mult).then_inc(gaps_ready, 1)

            def step_b(t, c):
                if runs(t, c, 2, SLOTS):
                    s, p = num(t, c - 2), (c - 2) % 2
                    dve.wait_ge(yslot_done, s + 1)
                    at_least(dve, back_done, s - 1)
                    nc.vector.tensor_scalar(yT_s[:, p, :], ps_y[:, :], w2_s[p][:, 2 * H:2 * H + 1].bitcast(F32), None,
                                            ALU.add).then_inc(yslotT_ready, 1)
                if runs(t, c, 0, SLOTS):
                    s, p = num(t, c), c % 2
                    for hc in range(HC):
                        dve.wait_ge(h_ready, HC * s + hc + 1)
                        nc.vector.tensor_copy(h_hi[p][hc][:, :], h_s[:, hc, :]).then_inc(hhi_ready, 1)
                        dve.wait_ge(hhi_ready, HC * s + hc + 1)
                        nc.vector.tensor_tensor(h_lo[p][hc][:, :], h_s[:, hc, :], h_hi[p][hc][:, :].bitcast(F32),
                                                ALU.subtract).then_inc(hlo_ready, 1)
                        if hc == HC - 2 and runs(t, c, -1, SLOTS):
                            x_low(t, c + 1)
                if runs(t, c, 0, SLOTS):
                    s, r = num(t, c), c % 4
                    dve.wait_ge(powers_ready, s + 1)
                    nc.vector.tensor_scalar(denom[:, :], powers[:, r, :, 0], 1.0, None, ALU.add).then_inc(denom_ready, 1)
                    dve.wait_ge(denom_ready, s + 1)
                    nc.vector.reciprocal(inverse[:, :], denom[:, :]).then_inc(inverse_ready, 1)
                    dve.wait_ge(inverse_ready, s + 1)
                    at_least(dve, y_weighted, s - 3)
                    nc.vector.tensor_tensor(weight[:, r, :], inverse[:, :], powers[:, r, :, 1], ALU.mult).then_inc(weight_ready, 1)

            x_low(0, 0)
            run_b(dve, step_b)

        @block.tensor
        def _(pe):
            pe.wait_ge(params_loaded, 16 * N_PARAMS)
            pe.wait_ge(pool_step, 8)
            pe.wait_ge(bias_ready, 1)

            def blk(bank_, b):
                return bank_[:, b * P:(b + 1) * P]

            def step(t, c):
                if runs(t, c, 3, GROUPS):
                    g, p, r = num(t, c - 3), (c - 3) % 2, (c - 3) % 4
                    pe.wait_ge(mask_ready, g + 1)
                    pe.wait_ge(seen_ready, g + 1)
                    at_least(pe, place_ready, g)
                    rank = ps_rank[:, 0:GB * E].rearrange("p (b e) -> p b e", b=GB)
                    nc.tensor.matmul(rank, before_bf[:, :], mask[:, p, :, :], start=True, stop=False)
                    for b in range(GB - 1):
                        nc.tensor.matmul(rank[:, b + 1:GB, :], ones_bf[:, :],
                                         mask[:, p, b, :].unsqueeze(1).to_broadcast([P, GB - 1 - b, E]), start=False, stop=False)
                    nc.tensor.matmul(rank, ones_bf[:, :], seen[:, r, :].unsqueeze(1).to_broadcast([P, GB, E]),
                                     start=False, stop=True).then_inc(rank_done, 1)
                if runs(t, c, 0, GROUPS):
                    g, p = num(t, c), c % 2
                    pe.wait_ge(n_ready, g + 1)
                    at_least(pe, hT_ready, g)
                    for b in range(GB):
                        last = nc.tensor.transpose(blk(ps_nT, b), n_s[:, p, b, :], ident[:, :])
                    last.then_inc(nT_done, 1)
                    pe.wait_ge(adj_loaded[p], 16 * uses(t, c, 2))
                    at_least(pe, adjT_ready, g)
                    for b in range(GB):
                        last = nc.tensor.transpose(blk(ps_adjT, b), adj_in[:, p, b, :], ident[:, :])
                    last.then_inc(adjT_done, 1)
                if runs(t, c, 2, GROUPS):
                    g, r = num(t, c - 2), (c - 2) % 4
                    pe.wait_ge(y_ready, g + 1)
                    at_least(pe, yT_ready, g)
                    for b in range(GB):
                        last = nc.tensor.transpose(blk(ps_yT, b), rows_s[:, r, b, 0:P], ident[:, :])
                    last.then_inc(yT_done, 1)
                if runs(t, c, 0, GROUPS):
                    g, p = num(t, c), c % 2
                    pe.wait_ge(hT_ready, g + 1)
                    at_least(pe, rel_ready, g)
                    for b in range(GB):
                        last = nc.tensor.matmul(blk(ps_rel, b), hT[:, p, b, :], w_rel_s[:, :], start=True, stop=True)
                    last.then_inc(rel_done, 1)
                if runs(t, c, 2, GROUPS):
                    g, p = num(t, c - 2), (c - 2) % 2
                    pe.wait_ge(yT_ready, g + 1)
                    at_least(pe, score_ready, g)
                    for b in range(GB):
                        last = nc.tensor.matmul(blk(ps_gate, b), yT[:, p, b, :], w_gate_s[:, :], start=True, stop=True)
                    last.then_inc(gate_done, 1)
                if runs(t, c, 0, GROUPS):
                    g, p = num(t, c), c % 2
                    at_least(pe, x1_ready, g - 1)
                    nc.tensor.matmul(ps_conv[p][:, :], ones_bf[:, :], b_rel3[:, :, :].rearrange("p b t -> p (b t)"), start=True, stop=False)
                    for b in range(GB):
                        nc.tensor.matmul(blk(ps_conv[p], b), hT[:, p, b, :], w_root_s[:, :], start=False, stop=False)
                if runs(t, c, 0, GROUPS):
                    g, p = num(t, c), c % 2
                    pe.wait_ge(rel_ready, g + 1)
                    pe.wait_ge(adjT_ready, g + 1)
                    for b in range(GB):
                        last = nc.tensor.matmul(blk(ps_conv[p], b), adjT[:, p, b, :], rel_s[:, p, b, :], start=False, stop=b == GB - 1)
                    last.then_inc(conv_done, 1)

            run_a(pe, step)

            pe.wait_ge(seen_ready, GROUPS + 1)
            pe.wait_ge(place_ready, GROUPS)
            nc.tensor.matmul(ps_rank[:, 0:E], ones_bf[:, :], seen[:, GROUPS % 4, :], start=True, stop=True).then_inc(lengths_done, 1)

            def x_turn(t, c):
                s, r = num(t, c), c % 4
                pe.wait_ge(xin_loaded[r], 16 * uses(t, c, 4))
                at_least(pe, xlo_ready, s)
                for j in range(SB):
                    last = nc.tensor.transpose(blk(ps_xT, j), xin[:, r, j, 0:P], ident[:, :])
                last.then_inc(xT_done, 1)

            def step_b(t, c):
                if runs(t, c, 0, SLOTS):
                    s, p = num(t, c), c % 2
                    pe.wait_ge(xlo_ready, s + 1)
                    pe.wait_ge(w1_loaded[p], 16 * uses(t, c, 2))
                    for hc in range(HC):
                        at_least(pe, h_ready, HC * (s - 1) + hc + 1)
                        high = w1_s[p][:, hc * P:(hc + 1) * P]
                        low = w1_s[p][:, H + hc * P:H + (hc + 1) * P]
                        nc.tensor.matmul(ps_h[hc][:, :], high, x_hi[p][:, :], start=True, stop=False)
                        nc.tensor.matmul(ps_h[hc][:, :], high, x_lo[p][:, :], start=False, stop=False)
                        nc.tensor.matmul(ps_h[hc][:, :], low, x_hi[p][:, :], start=False, stop=True).then_inc(h_done, 1)
                if runs(t, c, 2, SLOTS):
                    s, p = num(t, c - 2), (c - 2) % 2
                    pe.wait_ge(yslotT_ready, s + 1)
                    at_least(pe, y_weighted, s)
                    for j in range(SB):
                        last = nc.tensor.transpose(blk(ps_back, j), yT_s[:, p, j * P:(j + 1) * P], ident[:, :])
                    last.then_inc(back_done, 1)
                if runs(t, c, -1, SLOTS):
                    x_turn(t, c + 1)
                if runs(t, c, 1, SLOTS):
                    s, p = num(t, c - 1), (c - 1) % 2
                    pe.wait_ge(w2_loaded[p], 16 * uses(t, c - 1, 2))
                    at_least(pe, yslotT_ready, s)
                    for hc in range(HC):
                        pe.wait_ge(hlo_ready, HC * s + hc + 1)
                        high = w2_s[p][:, hc * P:(hc + 1) * P]
                        low = w2_s[p][:, H + hc * P:H + (hc + 1) * P]
                        nc.tensor.matmul(ps_y[:, :], high, h_hi[p][hc][:, :], start=hc == 0, stop=False)
                        nc.tensor.matmul(ps_y[:, :], high, h_lo[p][hc][:, :], start=False, stop=False)
                        last = nc.tensor.matmul(ps_y[:, :], low, h_hi[p][hc][:, :], start=False, stop=hc == HC - 1)
                    last.then_inc(yslot_done, 1)

            x_turn(0, 0)
            run_b(pe, step_b)


def kernel(x, adj, L0_gnn_W_rel, L0_gnn_b_rel, L0_gnn_W_root, L0_gnn_ln_gamma, L0_gnn_ln_beta,
           L0_ffn_Wg, L0_ffn_bg, L0_ffn_W1, L0_ffn_b1, L0_ffn_W2, L0_ffn_b2):
    import numpy as np
    import concourse.bacc as bacc
    from concourse.bass_utils import run_bass_kernel_spmd

    graphs, nodes, d = x.shape
    n_exp, hidden, _ = L0_ffn_W1.shape
    chunks = hidden // 128
    laid = {
        "x": x,
        "adj": adj,
        "w_rel": L0_gnn_W_rel,
        "b_rel": L0_gnn_b_rel,
        "w_root": L0_gnn_W_root,
        "gamma": np.reshape(L0_gnn_ln_gamma, (d, 1)),
        "beta": np.reshape(L0_gnn_ln_beta, (d, 1)),
        "w_gate": np.transpose(L0_ffn_Wg),
        "b_gate": L0_ffn_bg,
        "w1": np.transpose(L0_ffn_W1, (0, 2, 1)),
        "b1": np.transpose(np.reshape(L0_ffn_b1, (n_exp, chunks, 128)), (2, 0, 1)),
        "w2": np.reshape(np.transpose(np.reshape(L0_ffn_W2, (n_exp, d, chunks, 128)), (0, 3, 2, 1)), (n_exp, 128, hidden)),
        "b2": np.transpose(L0_ffn_b2),
    }
    nc = bacc.Bacc("TRN2", target_bir_lowering=False, num_devices=1)
    arrays, args = {}, []
    for name, a in laid.items():
        a = np.ascontiguousarray(a)
        arrays[f"in_{name}"] = a
        args.append(nc.dram_tensor(f"in_{name}", a.shape, mybir.dt.from_np(a.dtype), kind="ExternalInput").ap())
    tokens = graphs * nodes
    out = nc.dram_tensor("out_rows", [tokens + SPARE, d], F32, kind="ExternalOutput").ap()
    build_gnn_moe(nc, *args, out)
    r = run_bass_kernel_spmd(nc, [arrays], core_ids=[0])
    return np.reshape(r.results[0]["out_rows"][:tokens], (graphs, nodes, d))
```

```python
from contextlib import ExitStack

import concourse.bass as bass
from concourse import mybir

F32 = mybir.dt.float32
F32R = mybir.dt.float32r
BF16 = mybir.dt.bfloat16
I32 = mybir.dt.int32
U32 = mybir.dt.uint32
ALU = mybir.AluOpType
ACT = mybir.ActivationFunctionType
X = mybir.AxisListType.X

EPS = 1e-5
SPARE = 512


def build_gnn_moe(nc, x, adj, w_rel, b_rel, w_root, gamma, beta, w_gate, b_gate, w1, b1, w2, b2, out):
    P = 128
    GRAPHS = x.shape[0]
    T = GRAPHS * P
    GB = 4
    GROUPS = GRAPHS // GB
    E = w_gate.shape[1]
    TOP = 2
    H = w1.shape[2]
    HC = H // P
    SLOT = 512
    SB = SLOT // P
    SLOTS = TOP * T // SLOT + E - 1
    CAP = T + SLOT
    ROWS = E * CAP + SLOT
    META_ID, META_GAP, META_FIRST = P, P + 1, P + 2
    ROW = P + 4
    W1C, W2C = 2 * H + HC, 2 * H + 1
    TILES = T // SLOT

    routed = nc.dram_tensor("routed_rows", [ROWS, ROW], F32).ap()
    w1_split = nc.dram_tensor("w1_split", [E, P, W1C], F32).ap()
    w2_split = nc.dram_tensor("w2_split", [E, P, W2C], F32).ap()

    x_g = x.rearrange("(g b) t d -> g t b d", b=GB)
    adj_g = adj.rearrange("(g b) i j -> g i b j", b=GB)
    out_g = out[0:T, :].rearrange("(g b t) d -> g t b d", b=GB, t=P)

    with ExitStack() as ctx:
        def sb(name, shape, dt=F32):
            return ctx.enter_context(nc.sbuf_tensor(name, shape, dt))

        def sem(name):
            return ctx.enter_context(nc.semaphore(name))

        bank = [ctx.enter_context(nc.psum_tensor(f"bank{i}", [P, 512], F32)) for i in range(8)]
        ps_nT, ps_adjT, ps_rel, ps_conv, ps_yT, ps_gate, ps_rank = (bank[i] for i in range(7))
        ps_conv = [ps_conv, bank[7]]
        ps_h = bank[0:4]
        ps_xT, ps_y, ps_back = bank[4], bank[5], bank[6]

        ident = sb("ident", [P, P])
        ones_bf = sb("ones_bf", [P, P], BF16)
        before_bf = sb("before_bf", [P, P], BF16)
        w_rel_s = sb("w_rel_s", [P, P])
        w_root_s = sb("w_root_s", [P, P])
        gamma_s = sb("gamma_s", [P, 1])
        beta_s = sb("beta_s", [P, 1])
        w_gate_s = sb("w_gate_s", [P, P])
        b_both_s = sb("b_both_s", [P, P + E])
        b_part = sb("b_part", [P, 3, P + E], BF16)
        b_row = sb("b_row", [P, 3, P + E], BF16)
        b_rest = sb("b_rest", [P, 2, P + E])
        b_sum = sb("b_sum", [P, P + E], BF16)
        b_rel3 = sb("b_rel3", [P, GB, P], BF16)
        b_gate3 = sb("b_gate3", [P, GB, P], BF16)
        count_i = sb("count_i", [P, P], I32)
        expert_f = sb("expert_f", [P, E])
        base_f = sb("base_f", [P, E])
        tile_f = sb("tile_f", [P, TILES])
        slot_f = sb("slot_f", [P, SLOTS])
        order_f = sb("order_f", [P, E, E])
        ids = sb("ids", [P, GRAPHS], I32)
        fill = sb("fill", [P, SB, ROW])
        fill_id = sb("fill_id", [P, SB], I32)

        x_in = sb("x_in", [P, 2, GB, P])
        adj_in = sb("adj_in", [P, 2, GB, P])
        xstat = sb("xstat", [P, GB, 6])
        xmv = sb("xmv", [P, GB, 2])
        xvar = sb("xvar", [P, 2, GB])
        xroot = sb("xroot", [P, 2, GB])
        xr = sb("xr", [P, 2, GB])
        xscale = sb("xscale", [P, 2, GB])
        n_s = sb("n_s", [P, 2, GB, P])
        xl_s = sb("xl_s", [P, 2, GB, P])
        hT = sb("hT", [P, 2, GB, P])
        adjT = sb("adjT", [P, 2, GB, P])
        rel_s = sb("rel_s", [P, 2, GB, P])
        x1_s = sb("x1_s", [P, 2, GB, P])
        ystat = sb("ystat", [P, GB, 6])
        ymv = sb("ymv", [P, GB, 2])
        yvar = sb("yvar", [P, GB])
        yroot = sb("yroot", [P, GB])
        yr = sb("yr", [P, GB])
        yshift = sb("yshift", [P, GB])
        rows_s = sb("rows_s", [P, 4, GB, ROW])
        yT = sb("yT", [P, 2, GB, P])
        top8 = sb("top8", [P, GB, 8])
        which = sb("which", [P, GB, 8], U32)
        hot = sb("hot", [P, 2, GB, TOP, E])
        mask = sb("mask", [P, 2, GB, E], BF16)
        seen = sb("seen", [P, 4, E], BF16)
        seen_add = sb("seen_add", [P, E])
        place = sb("place", [P, GB, E])
        placed = sb("placed", [P, GB, TOP, E])
        place_f = sb("place_f", [P, GB, TOP])
        place_i = sb("place_i", [P, 4, GB, TOP], I32)

        w_raw = sb("w_raw", [P, 2, E, H])
        b1_raw = sb("b1_raw", [P, E, HC])
        b2_raw = sb("b2_raw", [P, E, 1])
        w1_sp = sb("w1_sp", [P, W1C])
        w2_sp = sb("w2_sp", [P, W2C])

        length = sb("length", [P, E])
        over = sb("over", [P, E, TILES])
        tiles = sb("tiles", [P, E])
        upto = sb("upto", [P, E])
        tri_t = sb("tri_t", [P, E, E])
        past = sb("past", [P, SLOTS, E])
        pasted = sb("pasted", [P, SLOTS, E])
        s_exp = sb("s_exp", [P, SLOTS])
        s_start = sb("s_start", [P, SLOTS])
        s_row = sb("s_row", [P, SLOTS])
        s_live = sb("s_live", [P, SLOTS])
        s_new = sb("s_new", [P, SLOTS])
        s_dead = sb("s_dead", [P, SLOTS])
        s_fence = sb("s_fence", [P, SLOTS])
        ends_f = sb("ends_f", [P, E])
        ends = sb("ends", [P, E], I32)
        table = sb("table", [P, SLOTS + 2, 8], I32)

        xin = sb("xin", [P, 4, SB, ROW])
        w1_s = [sb(f"w1_s{i}", [P, W1C], F32R) for i in range(2)]
        w2_s = [sb(f"w2_s{i}", [P, W2C], F32R) for i in range(2)]
        x_hi = [sb(f"x_hi{i}", [P, SLOT], F32R) for i in range(2)]
        x_lo = [sb(f"x_lo{i}", [P, SLOT], F32R) for i in range(2)]
        h_s = sb("h_s", [P, HC, SLOT])
        h_hi = [[sb(f"h_hi{i}{c}", [P, SLOT], F32R) for c in range(HC)] for i in range(2)]
        h_lo = [[sb(f"h_lo{i}{c}", [P, SLOT], F32R) for c in range(HC)] for i in range(2)]
        yT_s = sb("yT_s", [P, 2, SLOT])
        y_s = sb("y_s", [P, 4, SB, P])
        row_id = sb("row_id", [P, 4, SB], I32)
        gaps = sb("gaps", [P, 4, SB, 2])
        powers = sb("powers", [P, 4, SB, 2])
        denom = sb("denom", [P, SB])
        inverse = sb("inverse", [P, SB])
        weight = sb("weight", [P, 4, SB])

        params_loaded = sem("params_loaded")
        biases_loaded = sem("biases_loaded")
        waits_passed = sem("waits_passed")
        pool_step = sem("pool_step")
        consts_ready = sem("consts_ready")
        split_ready = sem("split_ready")
        bias_ready = sem("bias_ready")
        rows_picked = sem("rows_picked")
        dve_step = sem("dve_step")
        raw_loaded = sem("raw_loaded")
        w_high = sem("w_high")
        w_split = [sem(f"w{i + 1}_is_split") for i in range(2)]
        w_stored = [sem(f"w{i + 1}_stored") for i in range(2)]
        x_loaded = [sem(f"x_loaded{i}") for i in range(2)]
        adj_loaded = [sem(f"adj_loaded{i}") for i in range(2)]
        xstat_done = sem("xstat_done")
        xmv_done = sem("xmv_done")
        xvar_done = sem("xvar_done")
        xroot_done = sem("xroot_done")
        xinv_done = sem("xinv_done")
        xscale_done = sem("xscale_done")
        n_ready = sem("n_ready")
        xl_ready = sem("xl_ready")
        nT_done = sem("nT_done")
        adjT_done = sem("adjT_done")
        hT_ready = sem("hT_ready")
        adjT_ready = sem("adjT_ready")
        rel_done = sem("rel_done")
        rel_ready = sem("rel_ready")
        conv_done = sem("conv_done")
        x1_ready = sem("x1_ready")
        x1_stored = [sem(f"x1_stored{i}") for i in range(2)]
        ystat_done = sem("ystat_done")
        ymv_done = sem("ymv_done")
        yvar_done = sem("yvar_done")
        yroot_done = sem("yroot_done")
        yinv_done = sem("yinv_done")
        yscale_done = sem("yscale_done")
        y_ready = sem("y_ready")
        yT_done = sem("yT_done")
        yT_ready = sem("yT_ready")
        gate_done = sem("gate_done")
        top_ready = sem("top_ready")
        which_ready = sem("which_ready")
        hot_ready = sem("hot_ready")
        mask_ready = sem("mask_ready")
        added_ready = sem("added_ready")
        seen_ready = sem("seen_ready")
        rank_done = sem("rank_done")
        place_ready = sem("place_ready")
        placed_ready = sem("placed_ready")
        placef_ready = sem("placef_ready")
        meta_ready = sem("meta_ready")
        scattered = [sem(f"scattered{i}") for i in range(4)]
        lengths_done = sem("lengths_done")
        ends_ready = sem("ends_ready")
        table_ready = sem("table_ready")
        fill_stored = sem("fill_stored")

        xin_loaded = [sem(f"xin_loaded{i}") for i in range(4)]
        w1_loaded = [sem(f"w1_loaded{i}") for i in range(2)]
        w2_loaded = [sem(f"w2_loaded{i}") for i in range(2)]
        xT_done = sem("xT_done")
        xhi_ready = sem("xhi_ready")
        xlo_ready = sem("xlo_ready")
        gaps_ready = sem("gaps_ready")
        powers_ready = sem("powers_ready")
        denom_ready = sem("denom_ready")
        inverse_ready = sem("inverse_ready")
        weight_ready = sem("weight_ready")
        h_done = sem("h_done")
        h_ready = sem("h_ready")
        hhi_ready = sem("hhi_ready")
        hhi_last = sem("hhi_last")
        hlo_ready = sem("hlo_ready")
        yslot_done = sem("yslot_done")
        yslotT_ready = sem("yslotT_ready")
        back_done = sem("back_done")
        y_weighted = sem("y_weighted")
        added = [sem(f"added{i}") for i in range(4)]

        N_PARAMS = 5

        def at_least(eng, s, value):
            if isinstance(value, int) and value <= 0:
                return
            eng.wait_ge(s, value)

        def apart(eng):
            eng.sem_inc(waits_passed, 1)

        def num(t, c):
            return ROUND * t + c

        def uses(t, c, ring):
            return t * (ROUND // ring) + c // ring + 1

        def pipeline(eng, step, first_full, n, lag_end):
            rounds = (n - first_full) // ROUND
            for i in range(first_full):
                step(0, i)
            with eng.Fori(0, rounds) as t:
                for c in range(ROUND):
                    step(t, first_full + c)
            for i in range(first_full + ROUND * rounds, n + lag_end):
                step(0, i)

        def runs(t, c, lag, n):
            i = ROUND * t + c if isinstance(t, int) else None
            return i is None or 0 <= i - lag < n

        ROUND = 8
        A_FULL, A_LAG = 5, 2
        B_FULL, B_LAG = 9, 2
        B_LAST = SLOTS - 1

        def run_a(eng, step):
            pipeline(eng, step, A_FULL, GROUPS - 1, 1 + A_LAG)

        def run_b(eng, step):
            pipeline(eng, step, B_FULL, B_LAST, 1 + B_LAG)

        block = ctx.enter_context(nc.Block())

        @block.sync
        def _(sp):
            def load(t, c):
                g, p = num(t, c), c % 2
                at_least(sp, xl_ready, g - 1)
                at_least(sp, n_ready, g - 1)
                sp.dma_start(x_in[:, p, :, :], x_g[g]).then_inc(x_loaded[p], 16)
                at_least(sp, adjT_done, g - 1)
                sp.dma_start(adj_in[:, p, :, :], adj_g[g]).then_inc(adj_loaded[p], 16)

            def store(t, c):
                g, p = num(t, c), c % 2
                sp.wait_ge(x1_ready, g + 1)
                sp.dma_start(out_g[g], x1_s[:, p, :, :]).then_inc(x1_stored[p], 16)

            def load_params(*pairs):
                for dst, src in pairs:
                    sp.dma_start(dst, src).then_inc(params_loaded, 16)

            sp.dma_start(x_in[:, 0, :, :], x_g[0]).then_inc(x_loaded[0], 16)
            sp.dma_start(b_both_s[:, 0:P], b_rel.partition_broadcast(P)).then_inc(biases_loaded, 16)
            sp.dma_start(b_both_s[:, P:], b_gate.partition_broadcast(P)).then_inc(biases_loaded, 16)
            load_params((gamma_s[:, :], gamma), (beta_s[:, :], beta), (w_rel_s[:, :], w_rel), (w_root_s[:, :], w_root))
            sp.dma_start(adj_in[:, 0, :, :], adj_g[0]).then_inc(adj_loaded[0], 16)
            sp.wait_ge(consts_ready, 1)
            sp.dma_start(w_gate_s[:, 0:E], w_gate).then_inc(params_loaded, 16)

            half = E // 2
            raw_parts = [(w_raw[:, n, h:h + half, :], w[h:h + half].rearrange("e p c -> p e c"))
                         for n, w in enumerate((w1, w2)) for h in (0, half)]
            raw_parts += [(b1_raw[:, :, :], b1), (b2_raw[:, :, 0], b2)]

            def load_weights(parts):
                for dst, src in parts:
                    sp.dma_start(dst, src).then_inc(raw_loaded, 16)

            def store_weights(e, n):
                both, split = ((w1_sp, w1_split), (w2_sp, w2_split))[n]
                sp.wait_ge(w_split[n], e + 1)
                dst = split[e] if isinstance(e, int) else split[bass.ds(e, 1)].rearrange("a p c -> p (a c)")
                sp.dma_start(dst, both[:, :]).then_inc(w_stored[n], 16)

            def step(t, c):
                if runs(t, c, -1, GROUPS):
                    load(t, c + 1)
                if runs(t, c, 1, GROUPS):
                    store(t, c - 1)
                if isinstance(t, int) and c < 3:
                    load_weights(raw_parts[2 * c:2 * c + 2])
                if 4 <= c < 4 * E and c % 2 == 0:
                    store_weights(ROUND // 4 * t + c // 4 - 1, c % 4 // 2)

            pipeline(sp, step, 3, GROUPS - 1, 2)
            for n in range(2):
                store_weights(E - 1, n)

            sp.wait_ge(ends_ready, 1)
            BOUNDED = "part P's arithmetic keeps each value in the bounds that the shapes give"
            _, list_ends = nc.values_load_multi_w_load_instructions(
                ends[0:1, :], engines=[mybir.EngineType.SP], min_val=0, max_val=ROWS - SLOT, skip_runtime_bounds_check_because=BOUNDED)
            for end in list_ends:
                dst = routed[bass.ds(end, SLOT), :].rearrange("(j p) d -> p j d", p=P)
                sp.dma_start(dst, fill[:, :, :]).then_inc(fill_stored, 16)
            sp.dma_start(routed[E * CAP:ROWS, :].rearrange("(j p) d -> p j d", p=P),
                         fill[:, :, :]).then_inc(fill_stored, 16)
            sp.dma_start(out[T:T + SPARE, :].rearrange("(j p) d -> p j d", p=P),
                         fill[:, :, 0:P]).then_inc(fill_stored, 16)
            for n in range(2):
                sp.wait_ge(w_stored[n], 16 * E)
            sp.wait_ge(table_ready, 1)

            def read_table(t, c):
                s = num(t, c)
                at = slice(s + 2, s + 3) if isinstance(s, int) else bass.ds(s + 2, 1)
                _, (row, e1, new1, e2, new2) = nc.values_load_multi_w_load_instructions(
                    table[0:1, at, 0:5].rearrange("p a c -> p (a c)"), engines=[mybir.EngineType.SP], min_val=0, max_val=ROWS - SLOT,
                    skip_runtime_bounds_check_because=BOUNDED)
                e1, e2 = (nc.s_assert_within(e, 0, E - 1, skip_runtime_bounds_check_because=BOUNDED) for e in (e1, e2))
                new1, new2 = (nc.s_assert_within(n, 0, 1, skip_runtime_bounds_check_because=BOUNDED) for n in (new1, new2))
                return row, e1, new1, e2, new2

            def load_rows(t, c, row):
                s, r = num(t, c), c % 4
                at_least(sp, xT_done, s - 3)
                at_least(sp, gaps_ready, s - 3)
                src = routed[bass.ds(row, SLOT), :].rearrange("(j p) d -> p j d", p=P)
                sp.dma_start(xin[:, r, :, :], src).then_inc(xin_loaded[r], 16)

            def load_w1(t, c, e, new):
                s, p = num(t, c), c % 2
                at_least(sp, h_ready, HC * (s - 1))
                sp.dma_start(w1_s[p][:, :].bitcast(F32), w1_split[bass.ds(e, 1), :, :].rearrange("a p c -> p (a c)"),
                             cond=new).then_inc(w1_loaded[p], 16)

            def load_w2(t, c, e, new):
                s, p = num(t, c), c % 2
                at_least(sp, yslotT_ready, s - 1)
                sp.dma_start(w2_s[p][:, :].bitcast(F32), w2_split[bass.ds(e, 1), :, :].rearrange("a p c -> p (a c)"),
                             cond=new).then_inc(w2_loaded[p], 16)

            def step_b(t, c):
                row, e1, new1, e2, new2 = read_table(t, c)
                if runs(t, c, -2, SLOTS):
                    load_rows(t, c + 2, row)
                if runs(t, c, -1, SLOTS):
                    load_w1(t, c + 1, e1, new1)
                if runs(t, c, 0, SLOTS):
                    load_w2(t, c, e2, new2)

            row_0 = read_table(0, -2)[0]
            row_1, e_0, new_0, _, _ = read_table(0, -1)
            load_w1(0, 0, e_0, new_0)
            sp.wait_ge(fill_stored, 16 * (E + 2))
            for p in range(2):
                sp.wait_ge(x1_stored[p], 16 * (GROUPS // 2))
            for r in range(4):
                sp.wait_ge(scattered[r], 128 * (GROUPS // 4))
            load_rows(0, 0, row_0)
            load_rows(0, 1, row_1)
            pipeline(sp, step_b, 3, SLOTS - 2, 2)
            for r in range(4):
                sp.wait_ge(added[r], 64 * ((SLOTS + 3 - r) // 4))

        @block.gpsimd
        def _(pool):
            nc.gpsimd.memset(w_gate_s[:, :], 0.0).then_inc(consts_ready, 1)
            nc.gpsimd.memset(ident[:, :], 0.0).then_inc(pool_step, 1)
            nc.gpsimd.memset(ones_bf[:, :], 1.0).then_inc(pool_step, 1)
            nc.gpsimd.memset(fill[:, :, :], 0.0).then_inc(pool_step, 1)
            pool.wait_ge(pool_step, 3)
            nc.gpsimd.affine_select(out=ident[:, :], in_=ident[:, :], compare_op=ALU.not_equal, fill=1.0,
                                    base=0, pattern=[[-1, P]], channel_multiplier=1).then_inc(pool_step, 1)
            nc.gpsimd.affine_select(out=before_bf[:, :], in_=ones_bf[:, :], compare_op=ALU.is_gt, fill=0.0,
                                    base=0, pattern=[[1, P]], channel_multiplier=-1).then_inc(pool_step, 1)
            nc.gpsimd.iota(ids[:, :], pattern=[[P, GRAPHS]], base=0, channel_multiplier=1).then_inc(pool_step, 1)
            nc.gpsimd.iota(fill_id[:, :], pattern=[[P, SB]], base=T, channel_multiplier=1).then_inc(pool_step, 1)
            pool.wait_ge(pool_step, 7)
            nc.gpsimd.tensor_copy(fill[:, :, META_ID:META_ID + 1].bitcast(I32),
                                  fill_id[:, :].unsqueeze(2)).then_inc(pool_step, 1)
            made = 8
            for dst, n, pattern in ((expert_f[:, :], E, [[1, E]]), (base_f[:, :], E, [[CAP, E]]),
                                    (tile_f[:, :], TILES, [[SLOT, TILES]]), (slot_f[:, :], SLOTS, [[1, SLOTS]]),
                                    (order_f[:, :, :].rearrange("p e f -> p (e f)"), E * E, [[1, E], [-1, E]])):
                nc.gpsimd.iota(count_i[:, 0:n], pattern=pattern, base=0, channel_multiplier=0).then_inc(pool_step, 1)
                made += 1
                pool.wait_ge(pool_step, made)
                nc.gpsimd.tensor_copy(dst, count_i[:, 0:n]).then_inc(pool_step, 1)
                made += 1
                pool.wait_ge(pool_step, made)
            pool.wait_ge(split_ready, 1)
            for k in range(3):
                nc.gpsimd.affine_select(out=b_row[:, k, :], in_=b_part[:, k, :], compare_op=ALU.is_equal, fill=0.0,
                                        base=-k, pattern=[[0, P + E]], channel_multiplier=1).then_inc(rows_picked, 1)

            def step(t, c):
                if runs(t, c, 2, GROUPS):
                    g, r = num(t, c - 2), (c - 2) % 4
                    pool.wait_ge(meta_ready, g + 1)
                    apart(pool)
                    for b in range(GB):
                        for k in range(TOP):
                            pool.indirect_dma_start(
                                out=routed, out_offset=bass.IndirectOffsetOnAxis(ap=place_i[:, r, b, k:k + 1], axis=0),
                                in_=rows_s[:, r, b, :], in_offset=None).then_inc(scattered[r], 16)

            run_a(pool, step)

            def step_b(t, c):
                if runs(t, c, 2, SLOTS):
                    s, r = num(t, c - 2), (c - 2) % 4
                    pool.wait_ge(y_weighted, s + 1)
                    pool.wait_ge(gaps_ready, s + 1)
                    if isinstance(s, int):
                        for d in range(1, min(s, 3) + 1):
                            pool.wait_ge(added[(s - d) % 4], 64 * uses(0, s - d, 4))
                    else:
                        fence = pool.value_load(table[0:1, bass.ds(s, 1), 5:6].rearrange("p a c -> p (a c)"), min_val=0, max_val=64)
                        for d in range(1, 4):
                            k = c - 2 - d + 4
                            pool.wait_ge(added[k % 4], 64 * (uses(t, k, 4) - 2) + fence)
                    apart(pool)
                    for j in range(SB):
                        pool.indirect_dma_start(
                            out=out, out_offset=bass.IndirectOffsetOnAxis(
                                ap=row_id[:, r, j:j + 1], axis=0),
                            in_=y_s[:, r, j, :], in_offset=None, compute_op=ALU.add,
                            bounds_check=T + SPARE - 1).then_inc(added[r], 16)

            pool.wait_ge(table_ready, 1)
            run_b(pool, step_b)

        @block.scalar
        def _(act):
            def x_root(t, c):
                act.wait_ge(xvar_done, num(t, c) + 1)
                nc.scalar.activation(xroot[:, :, :], xvar[:, :, :], ACT.Sqrt).then_inc(xroot_done, 1)

            def step(t, c):
                if runs(t, c, 2, GROUPS):
                    g, p = num(t, c - 2), (c - 2) % 2
                    act.wait_ge(yT_done, g + 1)
                    at_least(act, gate_done, g - 1)
                    nc.scalar.activation(yT[:, p, :, :], ps_yT[:, :].rearrange("p (b t) -> p b t", b=GB),
                                         ACT.Copy).then_inc(yT_ready, 1)
                if runs(t, c, 0, GROUPS):
                    g, p = num(t, c), c % 2
                    act.wait_ge(nT_done, g + 1)
                    at_least(act, rel_done, g - 1)
                    at_least(act, conv_done, g - 1)
                    nc.scalar.activation(hT[:, p, :, :], ps_nT[:, :].rearrange("p (b t) -> p b t", b=GB),
                                         ACT.Identity, bias=beta_s[:, 0:1], scale=gamma_s[:, 0:1]).then_inc(hT_ready, 1)
                    act.wait_ge(adjT_done, g + 1)
                    nc.scalar.activation(adjT[:, p, :, :], ps_adjT[:, :].rearrange("p (b t) -> p b t", b=GB),
                                         ACT.Copy).then_inc(adjT_ready, 1)
                    act.wait_ge(rel_done, g + 1)
                    nc.scalar.activation(rel_s[:, p, :, :], ps_rel[:, :].rearrange("p (b t) -> p b t", b=GB),
                                         ACT.Copy).then_inc(rel_ready, 1)
                if runs(t, c, 1, GROUPS):
                    act.wait_ge(yvar_done, num(t, c - 1) + 1)
                    nc.scalar.activation(yroot[:, :], yvar[:, :], ACT.Sqrt).then_inc(yroot_done, 1)
                if runs(t, c, 0, GROUPS):
                    g, p = num(t, c), c % 2
                    act.wait_ge(xscale_done, g + 1)
                    act.wait_ge(x_loaded[p], 16 * uses(t, c, 2))
                    at_least(act, x1_ready, g - 1)
                    for b in range(GB):
                        last = nc.scalar.activation(xl_s[:, p, b, :], x_in[:, p, b, :], ACT.Identity,
                                                    bias=xscale[:, 1, b:b + 1], scale=xscale[:, 0, b:b + 1])
                    last.then_inc(xl_ready, 1)
                if runs(t, c, -1, GROUPS):
                    x_root(t, c + 1)
                if runs(t, c, 1, GROUPS):
                    g, p, r = num(t, c - 1), (c - 1) % 2, (c - 1) % 4
                    act.wait_ge(yscale_done, g + 1)
                    if not isinstance(g, int) or g >= 4:
                        at_least(act, scattered[r], 128 * (uses(t, c - 1, 4) - 1))
                    for b in range(GB):
                        last = nc.scalar.activation(rows_s[:, r, b, 0:P], x1_s[:, p, b, :], ACT.Identity,
                                                    bias=yshift[:, b:b + 1], scale=yr[:, b:b + 1])
                    last.then_inc(y_ready, 1)

            x_root(0, 0)
            act.wait_ge(params_loaded, 16 * N_PARAMS)
            run_a(act, step)

            def step_b(t, c):
                s = num(t, c)
                if runs(t, c, 2, SLOTS):
                    s2, p = num(t, c - 2), (c - 2) % 2
                    act.wait_ge(yslot_done, s2 + 1)
                    at_least(act, back_done, s2 - 1)
                    nc.scalar.activation(yT_s[:, p, :], ps_y[:, :], ACT.Identity,
                                         bias=w2_s[p][:, 2 * H:2 * H + 1].bitcast(F32)).then_inc(yslotT_ready, 1)
                if runs(t, c, 0, SLOTS):
                    x_powers(t, c)
                    p = c % 2
                    for hc in range(HC):
                        act.wait_ge(h_done, HC * s + hc + 1)
                        at_least(act, hlo_ready, HC * (s - 1) + hc + 1)
                        nc.scalar.activation(h_s[:, hc, :], ps_h[hc][:, :], ACT.Relu,
                                             bias=w1_s[p][:, 2 * H + hc:2 * H + hc + 1].bitcast(F32)).then_inc(h_ready, 1)
                    act.wait_ge(h_ready, HC * (s + 1))
                    at_least(act, yslot_done, s - 1)
                    nc.scalar.activation(h_hi[p][HC - 1][:, :], h_s[:, HC - 1, :], ACT.Copy).then_inc(hhi_last, 1)
                if runs(t, c, -1, SLOTS):
                    x_high(t, c + 1)
                if runs(t, c, 2, SLOTS):
                    s2, p, r = num(t, c - 2), (c - 2) % 2, (c - 2) % 4
                    act.wait_ge(back_done, s2 + 1)
                    act.wait_ge(weight_ready, s2 + 1)
                    if not isinstance(s2, int) or s2 >= 4:
                        at_least(act, added[r], 64 * (uses(t, c - 2, 4) - 1))
                    for j in range(SB):
                        last = nc.scalar.activation(y_s[:, r, j, :], ps_back[:, j * P:(j + 1) * P], ACT.Copy,
                                                    scale=weight[:, r, j:j + 1])
                    last.then_inc(y_weighted, 1)

            def x_high(t, c):
                s, p = num(t, c), c % 2
                act.wait_ge(xT_done, s + 1)
                at_least(act, h_done, HC * (s - 1))
                nc.scalar.activation(x_hi[p][:, :], ps_xT[:, :], ACT.Copy).then_inc(xhi_ready, 1)

            def x_powers(t, c):
                s, r = num(t, c), c % 4
                act.wait_ge(gaps_ready, s + 1)
                at_least(act, weight_ready, s - 3)
                nc.scalar.activation(powers[:, r, :, :], gaps[:, r, :, :], ACT.Exp).then_inc(powers_ready, 1)

            x_high(0, 0)
            run_b(act, step_b)

        @block.vector
        def _(dve):
            steps = [0]

            def link(ins):
                steps[0] += 1
                ins.then_inc(dve_step, 1)
                dve.wait_ge(dve_step, steps[0])

            def stage1_stats(t, c):
                g, p = num(t, c), c % 2
                dve.wait_ge(x_loaded[p], 16 * uses(t, c, 2))
                for b in range(GB):
                    last = nc.vector.bn_stats(xstat[:, b, :], x_in[:, p, b, :])
                last.then_inc(xstat_done, 1)

            def stage1_aggr(t, c):
                g = num(t, c)
                dve.wait_ge(xstat_done, g + 1)
                apart(dve)
                for b in range(GB):
                    last = nc.vector.bn_aggr(xmv[:, b, :], xstat[:, b, :])
                last.then_inc(xmv_done, 1)

            def stage1_var(t, c):
                g = num(t, c)
                dve.wait_ge(xmv_done, g + 1)
                at_least(dve, xroot_done, g)
                nc.vector.tensor_scalar(xvar[:, 0, :], xmv[:, :, 1], EPS, None, ALU.add)
                nc.vector.tensor_scalar(xvar[:, 1, :], xmv[:, :, 1], 1.0 + EPS, EPS * EPS, ALU.mult, ALU.add).then_inc(xvar_done, 1)

            def stage1(t, c):
                g, p = num(t, c), c % 2
                dve.wait_ge(xroot_done, g + 1)
                nc.vector.reciprocal(xr[:, :, :], xroot[:, :, :]).then_inc(xinv_done, 1)
                dve.wait_ge(xinv_done, g + 1)
                at_least(dve, xl_ready, g)
                nc.vector.tensor_scalar(xscale[:, 0, :], xr[:, 0, :], 1.0, None, ALU.add)
                nc.vector.scalar_tensor_tensor(out=xscale[:, 1, :], in0=xmv[:, :, 0], scalar=-1.0, in1=xr[:, 0, :],
                                               op0=ALU.mult, op1=ALU.mult).then_inc(xscale_done, 1)
                at_least(dve, nT_done, g - 1)
                for b in range(GB):
                    last = nc.vector.tensor_scalar(n_s[:, p, b, :], x_in[:, p, b, :], xmv[:, b, 0:1], xr[:, 1, b:b + 1],
                                                   ALU.subtract, ALU.mult)
                last.then_inc(n_ready, 1)

            def stage2_x1(t, c):
                g, p = num(t, c), c % 2
                dve.wait_ge(conv_done, g + 1)
                dve.wait_ge(xl_ready, g + 1)
                if not isinstance(g, int) or g >= 2:
                    at_least(dve, x1_stored[p], 16 * (uses(t, c, 2) - 1))
                at_least(dve, y_ready, g - 1)
                nc.vector.scalar_tensor_tensor(out=x1_s[:, p, :, :], in0=ps_conv[p][:, :].rearrange("p (b t) -> p b t", b=GB),
                                               scalar=0.0, in1=xl_s[:, p, :, :], op0=ALU.max, op1=ALU.add).then_inc(x1_ready, 1)

            def stage2_stats(t, c):
                g, p = num(t, c), c % 2
                dve.wait_ge(x1_ready, g + 1)
                for b in range(GB):
                    last = nc.vector.bn_stats(ystat[:, b, :], x1_s[:, p, b, :])
                last.then_inc(ystat_done, 1)

            def stage2_aggr(t, c):
                g = num(t, c)
                dve.wait_ge(ystat_done, g + 1)
                apart(dve)
                for b in range(GB):
                    last = nc.vector.bn_aggr(ymv[:, b, :], ystat[:, b, :])
                last.then_inc(ymv_done, 1)

            def stage2_var(t, c):
                dve.wait_ge(ymv_done, num(t, c) + 1)
                nc.vector.tensor_scalar(yvar[:, :], ymv[:, :, 1], EPS, None, ALU.add).then_inc(yvar_done, 1)

            def stage2_root(t, c):
                g = num(t, c)
                dve.wait_ge(yroot_done, g + 1)
                at_least(dve, y_ready, g)
                nc.vector.reciprocal(yr[:, :], yroot[:, :]).then_inc(yinv_done, 1)

            def stage2_shift(t, c):
                dve.wait_ge(yinv_done, num(t, c) + 1)
                nc.vector.scalar_tensor_tensor(out=yshift[:, :], in0=ymv[:, :, 0], scalar=-1.0, in1=yr[:, :],
                                               op0=ALU.mult, op1=ALU.mult).then_inc(yscale_done, 1)

            scores = ps_gate[:, :].rearrange("p (b e) -> p b e", b=GB)[:, :, 0:E]

            def stage3_top(t, c):
                dve.wait_ge(gate_done, num(t, c) + 1)
                apart(dve)
                for b in range(GB):
                    last = nc.vector.max(top8[:, b, :], scores[:, b, :])
                last.then_inc(top_ready, 1)

            def stage3_which(t, c):
                g, p, r = num(t, c), c % 2, c % 4
                dve.wait_ge(top_ready, g + 1)
                apart(dve)
                for b in range(GB):
                    last = nc.vector.max_index(which[:, b, :], top8[:, b, :], scores[:, b, :])
                last.then_inc(which_ready, 1)
                dve.wait_ge(y_ready, g + 1)
                nc.vector.tensor_tensor(rows_s[:, r, :, META_GAP], top8[:, :, 1], top8[:, :, 0], ALU.subtract)

            def stage3_float(t, c):
                g, r = num(t, c), c % 4
                dve.wait_ge(which_ready, g + 1)
                nc.vector.tensor_copy(rows_s[:, r, :, META_FIRST:META_FIRST + TOP], which[:, :, 0:TOP]).then_inc(hot_ready, 1)

            def stage3_hot(t, c):
                g, p, r = num(t, c), c % 2, c % 4
                dve.wait_ge(hot_ready, 2 * g + 1)
                nc.vector.tensor_tensor(hot[:, p, :, :, :],
                                        rows_s[:, r, :, META_FIRST:META_FIRST + TOP].unsqueeze(3).to_broadcast([P, GB, TOP, E]),
                                        expert_f[:, :].unsqueeze(1).unsqueeze(1).to_broadcast([P, GB, TOP, E]),
                                        ALU.is_equal).then_inc(hot_ready, 1)

            def stage3_mask(t, c):
                g, p = num(t, c), c % 2
                dve.wait_ge(hot_ready, 2 * g + 2)
                at_least(dve, rank_done, g - 1)
                nc.vector.tensor_tensor(mask[:, p, :, :], hot[:, p, :, 0, :], hot[:, p, :, 1, :], ALU.add).then_inc(mask_ready, 1)

            def stage3_add(t, c):
                g, p = num(t, c), c % 2
                dve.wait_ge(mask_ready, g + 1)
                nc.vector.tensor_reduce(seen_add[:, :], mask[:, p, :, :].rearrange("p b e -> p e b"), X, ALU.add).then_inc(added_ready, 1)

            def stage3_seen(t, c):
                g, r = num(t, c), c % 4
                dve.wait_ge(added_ready, g + 1)
                at_least(dve, rank_done, g - 2)
                nc.vector.tensor_tensor(seen[:, (r + 1) % 4, :], seen[:, r, :], seen_add[:, :], ALU.add).then_inc(seen_ready, 1)

            def stage4_place(t, c):
                dve.wait_ge(rank_done, num(t, c) + 1)
                nc.vector.tensor_tensor(place[:, :, :], ps_rank[:, 0:GB * E].rearrange("p (b e) -> p b e", b=GB),
                                        base_f[:, :].unsqueeze(1).to_broadcast([P, GB, E]), ALU.add).then_inc(place_ready, 1)

            def stage4_pick(t, c):
                g, p = num(t, c), c % 2
                dve.wait_ge(place_ready, g + 1)
                nc.vector.tensor_tensor(placed[:, :, :, :], hot[:, p, :, :, :],
                                        place[:, :, :].unsqueeze(2).to_broadcast([P, GB, TOP, E]), ALU.mult).then_inc(placed_ready, 1)

            def stage4_meta(t, c):
                g, r = num(t, c), c % 4
                ids_g = ids[:, GB * g:GB * g + GB] if isinstance(g, int) else ids[:, bass.ds(GB * g, GB)]
                nc.vector.tensor_copy(rows_s[:, r, :, META_ID].bitcast(I32), ids_g)
                dve.wait_ge(placed_ready, g + 1)
                nc.vector.tensor_reduce(place_f[:, :, :], placed[:, :, :, :], X, ALU.add).then_inc(placef_ready, 1)

            def stage4_int(t, c):
                g, r = num(t, c), c % 4
                dve.wait_ge(placef_ready, g + 1)
                nc.vector.tensor_copy(place_i[:, r, :, :], place_f[:, :, :]).then_inc(meta_ready, 1)

            stage1_stats(0, 0)
            stage1_aggr(0, 0)
            stage1_var(0, 0)
            stage1(0, 0)
            dve.wait_ge(biases_loaded, 32)
            link(nc.vector.tensor_copy(b_part[:, 0, :], b_both_s[:, :]))
            link(nc.vector.tensor_tensor(b_rest[:, 0, :], b_both_s[:, :], b_part[:, 0, :], ALU.subtract))
            link(nc.vector.tensor_copy(b_part[:, 1, :], b_rest[:, 0, :]))
            link(nc.vector.tensor_tensor(b_rest[:, 1, :], b_rest[:, 0, :], b_part[:, 1, :], ALU.subtract))
            nc.vector.tensor_copy(b_part[:, 2, :], b_rest[:, 1, :]).then_inc(split_ready, 1)
            nc.vector.memset(seen[:, 0, :], 0.0).then_inc(seen_ready, 1)
            dve.wait_ge(rows_picked, 3)
            link(nc.vector.tensor_tensor(b_sum[:, :], b_row[:, 0, :], b_row[:, 1, :], ALU.add))
            link(nc.vector.tensor_tensor(b_sum[:, :], b_sum[:, :], b_row[:, 2, :], ALU.add))
            nc.vector.tensor_copy(b_rel3[:, :, :], b_sum[:, 0:P].unsqueeze(1).to_broadcast([P, GB, P])).then_inc(bias_ready, 1)
            link(nc.vector.memset(b_gate3[:, :, :], 0.0))
            nc.vector.tensor_copy(b_gate3[:, :, 0:E], b_sum[:, P:].unsqueeze(1).to_broadcast([P, GB, E])).then_inc(bias_ready, 1)


            def step(t, c):
                def now(part, lag):
                    if runs(t, c, lag, GROUPS):
                        part(t, c - lag)

                if not isinstance(t, int) or c > 0:
                    now(stage1, 0)
                now(stage2_x1, 1)
                now(stage2_stats, 1)
                now(stage1_stats, -1)
                now(stage2_aggr, 1)
                now(stage1_aggr, -1)
                now(stage2_var, 1)
                now(stage1_var, -1)
                now(stage3_top, 2)
                now(stage3_which, 2)
                now(stage3_float, 2)
                now(stage2_root, 1)
                now(stage3_hot, 2)
                now(stage2_shift, 1)
                now(stage3_mask, 2)
                now(stage3_add, 2)
                now(stage3_seen, 2)
                if not isinstance(t, int):
                    split_weights(ROUND // 4 * t + (c - A_FULL) // 4 + 1, (c - A_FULL) % 4)
                elif A_FULL - 2 <= c < A_FULL:
                    for part in range(2):
                        split_weights(0, 2 * (c - A_FULL + 2) + part)
                elif c >= GROUPS - 2:
                    split_weights(E - 1, c - (GROUPS - 2))
                now(stage4_place, 2)
                now(stage4_pick, 2)
                now(stage4_meta, 2)
                now(stage4_int, 2)

            def split_weights(e, part):
                def of(whole):
                    return whole[:, e, :] if isinstance(e, int) else whole[:, bass.ds(e, 1), :].rearrange("p a c -> p (a c)")

                n, low = divmod(part, 2)
                both = (w1_sp, w2_sp)[n]
                raw = of(w_raw[:, n, :, :])
                if low:
                    dve.wait_ge(w_high, 2 * e + n + 1)
                    nc.vector.tensor_tensor(both[:, H:2 * H].bitcast(F32R), raw, both[:, 0:H], ALU.subtract).then_inc(w_split[n], 1)
                else:
                    dve.wait_ge(raw_loaded, 16 * 6)
                    at_least(dve, w_stored[n], 16 * e)
                    nc.vector.tensor_copy(both[:, 2 * H:], of((b1_raw, b2_raw)[n]))
                    nc.vector.tensor_copy(both[:, 0:H].bitcast(F32R), raw).then_inc(w_high, 1)

            run_a(dve, step)

            dve.wait_ge(lengths_done, 1)
            link(nc.vector.tensor_copy(length[:, :], ps_rank[:, 0:E]))
            link(nc.vector.tensor_tensor(ends_f[:, :], length[:, :], base_f[:, :], ALU.add))
            nc.vector.tensor_copy(ends[:, :], ends_f[:, :]).then_inc(ends_ready, 1)
            link(nc.vector.tensor_tensor(over[:, :, :], length[:, :].unsqueeze(2).to_broadcast([P, E, TILES]),
                                         tile_f[:, :].unsqueeze(1).to_broadcast([P, E, TILES]), ALU.is_gt))
            link(nc.vector.tensor_reduce(tiles[:, :], over[:, :, :], X, ALU.add))
            link(nc.vector.tensor_scalar(tri_t[:, :, :], order_f[:, :, :], 0.0, None, ALU.is_ge))
            link(nc.vector.tensor_tensor(tri_t[:, :, :], tri_t[:, :, :], tiles[:, :].unsqueeze(1).to_broadcast([P, E, E]), ALU.mult))
            link(nc.vector.tensor_reduce(upto[:, :], tri_t[:, :, :], X, ALU.add))
            link(nc.vector.tensor_tensor(past[:, :, :], slot_f[:, :].unsqueeze(2).to_broadcast([P, SLOTS, E]),
                                         upto[:, :].unsqueeze(1).to_broadcast([P, SLOTS, E]), ALU.is_ge))
            link(nc.vector.tensor_reduce(s_exp[:, :], past[:, :, :], X, ALU.add))
            link(nc.vector.tensor_tensor(pasted[:, :, :], past[:, :, :], tiles[:, :].unsqueeze(1).to_broadcast([P, SLOTS, E]), ALU.mult))
            link(nc.vector.tensor_reduce(s_start[:, :], pasted[:, :, :], X, ALU.add))
            link(nc.vector.tensor_scalar(s_live[:, :], s_exp[:, :], float(E), float(SLOT), ALU.is_lt, ALU.mult))
            link(nc.vector.tensor_tensor(s_row[:, :], slot_f[:, :], s_start[:, :], ALU.subtract))
            link(nc.vector.tensor_tensor(s_row[:, :], s_row[:, :], s_live[:, :], ALU.mult))
            link(nc.vector.scalar_tensor_tensor(out=s_row[:, :], in0=s_exp[:, :], scalar=float(CAP), in1=s_row[:, :],
                                                op0=ALU.mult, op1=ALU.add))
            nc.vector.memset(s_fence[:, 0:1], 1.0)
            nc.vector.tensor_tensor(s_fence[:, 1:SLOTS], s_exp[:, 1:SLOTS], s_exp[:, 0:SLOTS - 1], ALU.not_equal)
            link(nc.vector.tensor_scalar(s_dead[:, :], s_exp[:, :], float(E), None, ALU.is_ge))
            link(nc.vector.tensor_tensor(s_fence[:, :], s_fence[:, :], s_dead[:, :], ALU.max))
            link(nc.vector.tensor_scalar(s_exp[:, :], s_exp[:, :], float(E - 1), None, ALU.min))
            nc.vector.memset(s_new[:, 0:2], 1.0)
            link(nc.vector.tensor_tensor(s_new[:, 2:SLOTS], s_exp[:, 2:SLOTS], s_exp[:, 0:SLOTS - 2], ALU.not_equal))
            link(nc.vector.memset(table[:, :, :], 0))
            nc.vector.tensor_copy(table[:, 0:SLOTS, 0], s_row[:, :])
            nc.vector.tensor_scalar(table[:, 0:SLOTS, 5], s_fence[:, :], 64.0, None, ALU.mult)
            nc.vector.tensor_copy(table[:, 1:SLOTS + 1, 1], s_exp[:, :])
            nc.vector.tensor_copy(table[:, 1:SLOTS + 1, 2], s_new[:, :])
            nc.vector.tensor_copy(table[:, 2:SLOTS + 2, 3], s_exp[:, :])
            nc.vector.tensor_copy(table[:, 2:SLOTS + 2, 4], s_new[:, :]).then_inc(table_ready, 1)

            def x_low(t, c):
                s, p = num(t, c), c % 2
                dve.wait_ge(xhi_ready, s + 1)
                at_least(dve, h_done, HC * (s - 1))
                nc.vector.tensor_tensor(x_lo[p][:, :], ps_xT[:, :], x_hi[p][:, :].bitcast(F32), ALU.subtract).then_inc(xlo_ready, 1)
                r = c % 4
                dve.wait_ge(xin_loaded[r], 16 * uses(t, c, 4))
                if not isinstance(s, int) or s >= 4:
                    at_least(dve, added[r], 64 * (uses(t, c, 4) - 1))
                nc.vector.tensor_copy(row_id[:, r, :], xin[:, r, :, META_ID].bitcast(I32))
                nc.vector.tensor_copy(gaps[:, r, :, 0], xin[:, r, :, META_GAP])
                own = s_exp[:, s:s + 1] if isinstance(s, int) else s_exp[:, bass.ds(s, 1)]
                nc.vector.scalar_tensor_tensor(out=gaps[:, r, :, 1], in0=xin[:, r, :, META_FIRST], scalar=own, in1=xin[:, r, :, META_GAP],
                                               op0=ALU.not_equal, op1=ALU.mult).then_inc(gaps_ready, 1)

            def step_b(t, c):
                if runs(t, c, 0, SLOTS):
                    s, p = num(t, c), c % 2
                    for hc in range(HC):
                        dve.wait_ge(h_ready, HC * s + hc + 1)
                        if hc < HC - 1:
                            nc.vector.tensor_copy(h_hi[p][hc][:, :], h_s[:, hc, :]).then_inc(hhi_ready, 1)
                            dve.wait_ge(hhi_ready, (HC - 1) * s + hc + 1)
                        else:
                            dve.wait_ge(hhi_last, s + 1)
                        nc.vector.tensor_tensor(h_lo[p][hc][:, :], h_s[:, hc, :], h_hi[p][hc][:, :].bitcast(F32),
                                                ALU.subtract).then_inc(hlo_ready, 1)
                        if hc == HC - 2 and runs(t, c, -1, SLOTS):
                            x_low(t, c + 1)
                if runs(t, c, 0, SLOTS):
                    s, r = num(t, c), c % 4
                    dve.wait_ge(powers_ready, s + 1)
                    nc.vector.tensor_scalar(denom[:, :], powers[:, r, :, 0], 1.0, None, ALU.add).then_inc(denom_ready, 1)
                    dve.wait_ge(denom_ready, s + 1)
                    nc.vector.reciprocal(inverse[:, :], denom[:, :]).then_inc(inverse_ready, 1)
                    dve.wait_ge(inverse_ready, s + 1)
                    at_least(dve, y_weighted, s - 3)
                    nc.vector.tensor_tensor(weight[:, r, :], inverse[:, :], powers[:, r, :, 1], ALU.mult).then_inc(weight_ready, 1)

            x_low(0, 0)
            run_b(dve, step_b)

        @block.tensor
        def _(pe):
            pe.wait_ge(params_loaded, 16 * N_PARAMS)
            pe.wait_ge(pool_step, 8)

            def blk(bank_, b):
                return bank_[:, b * P:(b + 1) * P]

            def step(t, c):
                if runs(t, c, 2, GROUPS):
                    g, r = num(t, c - 2), (c - 2) % 4
                    pe.wait_ge(y_ready, g + 1)
                    at_least(pe, yT_ready, g)
                    for b in range(GB):
                        last = nc.tensor.transpose(blk(ps_yT, b), rows_s[:, r, b, 0:P], ident[:, :])
                    last.then_inc(yT_done, 1)
                if runs(t, c, 0, GROUPS):
                    g, p = num(t, c), c % 2
                    pe.wait_ge(n_ready, g + 1)
                    at_least(pe, hT_ready, g)
                    for b in range(GB):
                        last = nc.tensor.transpose(blk(ps_nT, b), n_s[:, p, b, :], ident[:, :])
                    last.then_inc(nT_done, 1)
                    pe.wait_ge(adj_loaded[p], 16 * uses(t, c, 2))
                    at_least(pe, adjT_ready, g)
                    for b in range(GB):
                        last = nc.tensor.transpose(blk(ps_adjT, b), adj_in[:, p, b, :], ident[:, :])
                    last.then_inc(adjT_done, 1)
                if runs(t, c, 2, GROUPS):
                    g, p = num(t, c - 2), (c - 2) % 2
                    pe.wait_ge(yT_ready, g + 1)
                    at_least(pe, which_ready, g)
                    nc.tensor.matmul(ps_gate[:, :], ones_bf[:, :], b_gate3[:, :, :].rearrange("p b e -> p (b e)"), start=True, stop=False)
                    for b in range(GB):
                        last = nc.tensor.matmul(blk(ps_gate, b), yT[:, p, b, :], w_gate_s[:, :], start=False, stop=b == GB - 1)
                    last.then_inc(gate_done, 1)
                if runs(t, c, 0, GROUPS):
                    g, p = num(t, c), c % 2
                    pe.wait_ge(hT_ready, g + 1)
                    at_least(pe, rel_ready, g)
                    for b in range(GB):
                        last = nc.tensor.matmul(blk(ps_rel, b), hT[:, p, b, :], w_rel_s[:, :], start=True, stop=True)
                    last.then_inc(rel_done, 1)
                if runs(t, c, 0, GROUPS):
                    g, p = num(t, c), c % 2
                    at_least(pe, x1_ready, g - 1)
                    if isinstance(t, int) and c == 0:
                        pe.wait_ge(bias_ready, 2)
                    nc.tensor.matmul(ps_conv[p][:, :], ones_bf[:, :], b_rel3[:, :, :].rearrange("p b t -> p (b t)"), start=True, stop=False)
                    for b in range(GB):
                        nc.tensor.matmul(blk(ps_conv[p], b), hT[:, p, b, :], w_root_s[:, :], start=False, stop=False)
                if runs(t, c, 2, GROUPS):
                    g, p, r = num(t, c - 2), (c - 2) % 2, (c - 2) % 4
                    pe.wait_ge(mask_ready, g + 1)
                    pe.wait_ge(seen_ready, g + 1)
                    at_least(pe, place_ready, g)
                    rank = ps_rank[:, 0:GB * E].rearrange("p (b e) -> p b e", b=GB)
                    nc.tensor.matmul(rank, before_bf[:, :], mask[:, p, :, :], start=True, stop=False)
                    for b in range(GB - 1):
                        nc.tensor.matmul(rank[:, b + 1:GB, :], ones_bf[:, :],
                                         mask[:, p, b, :].unsqueeze(1).to_broadcast([P, GB - 1 - b, E]), start=False, stop=False)
                    nc.tensor.matmul(rank, ones_bf[:, :], seen[:, r, :].unsqueeze(1).to_broadcast([P, GB, E]),
                                     start=False, stop=True).then_inc(rank_done, 1)
                if runs(t, c, 0, GROUPS):
                    g, p = num(t, c), c % 2
                    pe.wait_ge(rel_ready, g + 1)
                    pe.wait_ge(adjT_ready, g + 1)
                    for b in range(GB):
                        last = nc.tensor.matmul(blk(ps_conv[p], b), adjT[:, p, b, :], rel_s[:, p, b, :], start=False, stop=b == GB - 1)
                    last.then_inc(conv_done, 1)

            run_a(pe, step)

            pe.wait_ge(seen_ready, GROUPS + 1)
            pe.wait_ge(place_ready, GROUPS)
            nc.tensor.matmul(ps_rank[:, 0:E], ones_bf[:, :], seen[:, GROUPS % 4, :], start=True, stop=True).then_inc(lengths_done, 1)

            def x_turn(t, c):
                s, r = num(t, c), c % 4
                pe.wait_ge(xin_loaded[r], 16 * uses(t, c, 4))
                at_least(pe, xlo_ready, s)
                for j in range(SB):
                    last = nc.tensor.transpose(blk(ps_xT, j), xin[:, r, j, 0:P], ident[:, :])
                last.then_inc(xT_done, 1)

            def step_b(t, c):
                if runs(t, c, 0, SLOTS):
                    s, p = num(t, c), c % 2
                    pe.wait_ge(xlo_ready, s + 1)
                    pe.wait_ge(w1_loaded[p], 16 * uses(t, c, 2))
                    for hc in range(HC):
                        at_least(pe, h_ready, HC * (s - 1) + hc + 1)
                        high = w1_s[p][:, hc * P:(hc + 1) * P]
                        low = w1_s[p][:, H + hc * P:H + (hc + 1) * P]
                        nc.tensor.matmul(ps_h[hc][:, :], high, x_hi[p][:, :], start=True, stop=False)
                        nc.tensor.matmul(ps_h[hc][:, :], high, x_lo[p][:, :], start=False, stop=False)
                        nc.tensor.matmul(ps_h[hc][:, :], low, x_hi[p][:, :], start=False, stop=True).then_inc(h_done, 1)
                if runs(t, c, 2, SLOTS):
                    s, p = num(t, c - 2), (c - 2) % 2
                    pe.wait_ge(yslotT_ready, s + 1)
                    at_least(pe, y_weighted, s)
                    for j in range(SB):
                        last = nc.tensor.transpose(blk(ps_back, j), yT_s[:, p, j * P:(j + 1) * P], ident[:, :])
                    last.then_inc(back_done, 1)
                if runs(t, c, -1, SLOTS):
                    x_turn(t, c + 1)
                if runs(t, c, 1, SLOTS):
                    s, p = num(t, c - 1), (c - 1) % 2
                    pe.wait_ge(w2_loaded[p], 16 * uses(t, c - 1, 2))
                    at_least(pe, yslotT_ready, s)
                    for hc in range(HC):
                        pe.wait_ge(hlo_ready, HC * s + hc + 1)
                        high = w2_s[p][:, hc * P:(hc + 1) * P]
                        low = w2_s[p][:, H + hc * P:H + (hc + 1) * P]
                        nc.tensor.matmul(ps_y[:, :], high, h_hi[p][hc][:, :], start=hc == 0, stop=False)
                        nc.tensor.matmul(ps_y[:, :], high, h_lo[p][hc][:, :], start=False, stop=False)
                        last = nc.tensor.matmul(ps_y[:, :], low, h_hi[p][hc][:, :], start=False, stop=hc == HC - 1)
                    last.then_inc(yslot_done, 1)

            x_turn(0, 0)
            run_b(pe, step_b)


def kernel(x, adj, L0_gnn_W_rel, L0_gnn_b_rel, L0_gnn_W_root, L0_gnn_ln_gamma, L0_gnn_ln_beta,
           L0_ffn_Wg, L0_ffn_bg, L0_ffn_W1, L0_ffn_b1, L0_ffn_W2, L0_ffn_b2):
    import numpy as np
    import concourse.bacc as bacc
    from concourse.bass_utils import run_bass_kernel_spmd

    graphs, nodes, d = x.shape
    n_exp, hidden, _ = L0_ffn_W1.shape
    chunks = hidden // 128
    laid = {
        "x": x,
        "adj": adj,
        "w_rel": L0_gnn_W_rel,
        "b_rel": L0_gnn_b_rel,
        "w_root": L0_gnn_W_root,
        "gamma": np.reshape(L0_gnn_ln_gamma, (d, 1)),
        "beta": np.reshape(L0_gnn_ln_beta, (d, 1)),
        "w_gate": np.transpose(L0_ffn_Wg),
        "b_gate": L0_ffn_bg,
        "w1": np.transpose(L0_ffn_W1, (0, 2, 1)),
        "b1": np.transpose(np.reshape(L0_ffn_b1, (n_exp, chunks, 128)), (2, 0, 1)),
        "w2": np.reshape(np.transpose(np.reshape(L0_ffn_W2, (n_exp, d, chunks, 128)), (0, 3, 2, 1)), (n_exp, 128, hidden)),
        "b2": np.transpose(L0_ffn_b2),
    }
    nc = bacc.Bacc("TRN2", target_bir_lowering=False, num_devices=1)
    arrays, args = {}, []
    for name, a in laid.items():
        a = np.ascontiguousarray(a)
        arrays[f"in_{name}"] = a
        args.append(nc.dram_tensor(f"in_{name}", a.shape, mybir.dt.from_np(a.dtype), kind="ExternalInput").ap())
    tokens = graphs * nodes
    out = nc.dram_tensor("out_rows", [tokens + SPARE, d], F32, kind="ExternalOutput").ap()
    build_gnn_moe(nc, *args, out)
    r = run_bass_kernel_spmd(nc, [arrays], core_ids=[0])
    return np.reshape(r.results[0]["out_rows"][:tokens], (graphs, nodes, d))
```
